# Optimizing a Trainium2 kernel written in Bass

```python
import numpy as np
import jax
import jax.numpy as jnp

def _softmax(x, axis=-1):
    return jax.nn.softmax(x, axis=axis)

def _gelu(x):
    return jax.nn.gelu(x, approximate=True)

def _silu(x):
    return jax.nn.silu(x)

def _sigmoid(x):
    return jax.nn.sigmoid(x)

def _layernorm(x, axis=-1, eps=1e-05):
    m = jnp.mean(x, axis=axis, keepdims=True)
    v = jnp.var(x, axis=axis, keepdims=True)
    return (x - m) / jnp.sqrt(v + eps)

def _scatter_add(tgt, idx, src, axis=0):
    return tgt.at[idx].add(src)

def _segment_sum(src, seg, n):
    return jax.ops.segment_sum(src, seg, n)
kernel_name = 'mk_xattn_ffn_d1_seqx_r8_85533e'

def setup_inputs(seed: int=0):
    np.random.seed(seed)
    _w = jnp.asarray

    def _rec_inputs():
        import jax
        import jax.numpy as jnp
        _rk = jax.random.key(seed)
        x = -0.000125 + 0.9999 * jax.random.normal(jax.random.fold_in(_rk, 1), (8, 128, 128), jnp.float32)
        _lenS = 128 - jax.random.randint(jax.random.fold_in(_rk, 7), (8,), 0, max(1, 128 // 4) + 1, jnp.int32)
        _lenS2 = 128 - jax.random.randint(jax.random.fold_in(_rk, 8), (8,), 0, max(1, 128 // 4) + 1, jnp.int32)
        _ctx_1024P = jax.random.normal(jax.random.fold_in(_rk, 11), (8, 16, 128), jnp.float32)
        _ctx_1024c = jax.random.dirichlet(jax.random.fold_in(_rk, 511), 0.3 * jnp.ones((16,), jnp.float32), (8, 128))
        _ctx_1024t = jnp.einsum('bsk,bkd->bsd', _ctx_1024c, _ctx_1024P)
        _ctx_1024t = _ctx_1024t * jax.lax.rsqrt(jnp.mean(jnp.square(_ctx_1024t)) + 1e-12) * 0.953939
        ctx_1024 = -1.52775e-05 + 0.999936 * (_ctx_1024t + 0.3 * jax.random.normal(jax.random.fold_in(_rk, 611), (8, 128, 128), jnp.float32))
        return (x, ctx_1024)
    x, ctx_1024 = _rec_inputs()

    def _L0_xattn_setup():
        import jax, jax.numpy as jnp
        import numpy as np
        N_HEADS = 4
        IN_FEATURES = 128

        def _channel_attention(qm, km, vm, scale):
            b, n, c = qm.shape
            d = c // N_HEADS
            qh = qm.reshape(b, n, N_HEADS, d).transpose(0, 2, 3, 1)
            kh = km.reshape(b, n, N_HEADS, d).transpose(0, 2, 3, 1)
            vh = vm.reshape(b, n, N_HEADS, d).transpose(0, 2, 3, 1)
            scores = jnp.einsum('bhdn,bhen->bhde', qh, kh) * scale
            attn = jax.nn.softmax(scores, axis=-1)
            out = jnp.einsum('bhde,bhen->bhdn', attn, vh)
            return out.transpose(0, 3, 1, 2).reshape(b, n, c)
        key = jax.random.key(seed)
        ks = jax.random.split(key, 20)
        B, HW, C = (2, 2048, 128)
        inp = {'q': jax.random.normal(ks[0], (B, HW, C), dtype=jnp.float32), 'k': jax.random.normal(ks[1], (B, HW, C), dtype=jnp.float32), 'v': jax.random.normal(ks[2], (B, HW, C), dtype=jnp.float32)}
        names = ['wqg', 'bqg', 'wkg', 'bkg', 'wvg', 'bvg', 'wql', 'bql', 'wkl', 'bkl', 'wvl', 'bvl', 'wp', 'bp']
        for i, n in enumerate(names):
            inp[n] = jax.random.normal(ks[3 + i], (C,), dtype=jnp.float32)
        return inp
    _L0_xattn_all = _L0_xattn_setup()
    _L0_xattn_in = {k: v for k, v in _L0_xattn_all.items() if k in ('wqg', 'bqg', 'wkg', 'bkg', 'wvg', 'bvg', 'wql', 'bql', 'wkl', 'bkl', 'wvl', 'bvl', 'wp', 'bp')}
    del _L0_xattn_all

    def _L0_ffn_setup():
        import jax, jax.numpy as jnp
        import numpy as np
        B, S, D, F, E, K = (4, 256, 128, 512, 8, 2)
        key = jax.random.key(seed)
        ks = jax.random.split(key, 8)
        x = jax.random.normal(ks[0], (B, S, D), dtype=jnp.float32)
        router_w = jax.random.normal(ks[1], (E, D), dtype=jnp.float32) * 0.02
        w1_w = jax.random.normal(ks[2], (E, F, D), dtype=jnp.float32) * 0.02
        w1_b = jax.random.normal(ks[3], (E, F), dtype=jnp.float32) * 0.02
        w2_w = jax.random.normal(ks[4], (E, D, F), dtype=jnp.float32) * 0.02
        w2_b = jax.random.normal(ks[5], (E, D), dtype=jnp.float32) * 0.02
        wg_w = jax.random.normal(ks[6], (E, F, D), dtype=jnp.float32) * 0.02
        wg_b = jax.random.normal(ks[7], (E, F), dtype=jnp.float32) * 0.02
        return {'x': x, 'router_w': router_w, 'w1_w': w1_w, 'w1_b': w1_b, 'w2_w': w2_w, 'w2_b': w2_b, 'wg_w': wg_w, 'wg_b': wg_b}
    _L0_ffn_all = _L0_ffn_setup()
    _L0_ffn_in = {k: v for k, v in _L0_ffn_all.items() if k in ('router_w', 'w1_w', 'w1_b', 'w2_w', 'w2_b', 'wg_w', 'wg_b')}
    del _L0_ffn_all
    return {'x': x, 'ctx_1024': ctx_1024, 'L0_xattn_wqg': _L0_xattn_in['wqg'], 'L0_xattn_bqg': _L0_xattn_in['bqg'], 'L0_xattn_wkg': _L0_xattn_in['wkg'], 'L0_xattn_bkg': _L0_xattn_in['bkg'], 'L0_xattn_wvg': _L0_xattn_in['wvg'], 'L0_xattn_bvg': _L0_xattn_in['bvg'], 'L0_xattn_wql': _L0_xattn_in['wql'], 'L0_xattn_bql': _L0_xattn_in['bql'], 'L0_xattn_wkl': _L0_xattn_in['wkl'], 'L0_xattn_bkl': _L0_xattn_in['bkl'], 'L0_xattn_wvl': _L0_xattn_in['wvl'], 'L0_xattn_bvl': _L0_xattn_in['bvl'], 'L0_xattn_wp': _L0_xattn_in['wp'], 'L0_xattn_bp': _L0_xattn_in['bp'], 'L0_ffn_router_w': _L0_ffn_in['router_w'], 'L0_ffn_w1_w': _L0_ffn_in['w1_w'], 'L0_ffn_w1_b': _L0_ffn_in['w1_b'], 'L0_ffn_w2_w': _L0_ffn_in['w2_w'], 'L0_ffn_w2_b': _L0_ffn_in['w2_b'], 'L0_ffn_wg_w': _L0_ffn_in['wg_w'], 'L0_ffn_wg_b': _L0_ffn_in['wg_b']}

def reference(x, ctx_1024, L0_xattn_wqg, L0_xattn_bqg, L0_xattn_wkg, L0_xattn_bkg, L0_xattn_wvg, L0_xattn_bvg, L0_xattn_wql, L0_xattn_bql, L0_xattn_wkl, L0_xattn_bkl, L0_xattn_wvl, L0_xattn_bvl, L0_xattn_wp, L0_xattn_bp, L0_ffn_router_w, L0_ffn_w1_w, L0_ffn_w1_b, L0_ffn_w2_w, L0_ffn_w2_b, L0_ffn_wg_w, L0_ffn_wg_b):
    import jax
    import jax.numpy as jnp

    def _L0_xattn_ref(q, k, v, wqg, bqg, wkg, bkg, wvg, bvg, wql, bql, wkl, bkl, wvl, bvl, wp, bp):
        import jax, jax.numpy as jnp
        import numpy as np
        N_HEADS = 4
        IN_FEATURES = 128

        def _channel_attention(qm, km, vm, scale):
            b, n, c = qm.shape
            d = c // N_HEADS
            qh = qm.reshape(b, n, N_HEADS, d).transpose(0, 2, 3, 1)
            kh = km.reshape(b, n, N_HEADS, d).transpose(0, 2, 3, 1)
            vh = vm.reshape(b, n, N_HEADS, d).transpose(0, 2, 3, 1)
            scores = jnp.einsum('bhdn,bhen->bhde', qh, kh) * scale
            attn = jax.nn.softmax(scores, axis=-1)
            out = jnp.einsum('bhde,bhen->bhdn', attn, vh)
            return out.transpose(0, 3, 1, 2).reshape(b, n, c)
        scale = IN_FEATURES ** (-0.5)
        att_global = _channel_attention(q * wqg + bqg, k * wkg + bkg, v * wvg + bvg, scale)
        att_local = _channel_attention(q * wql + bql, k * wkl + bkl, v * wvl + bvl, scale)
        att = att_global + att_local
        return 2.0 * att * wp + bp

    def _L0_ffn_ref(x, router_w, w1_w, w1_b, w2_w, w2_b, wg_w, wg_b):
        import jax, jax.numpy as jnp
        import numpy as np
        B, S, D, F, E, K = (4, 256, 128, 512, 8, 2)
        probs = jax.nn.softmax(jnp.einsum('bsd,ed->bse', x, router_w), axis=-1)
        token_probs, probs_idx = jax.lax.top_k(probs, K)
        gates = jnp.sum(token_probs[..., None] * jax.nn.one_hot(probs_idx, E, dtype=x.dtype), axis=-2)
        gates_e = jnp.moveaxis(gates, -1, 0)

        def body(acc, params):
            w1w, w1b, w2w, w2b, wgw, wgb, g = params
            y = jax.nn.gelu(jnp.einsum('bsd,fd->bsf', x, wgw) + wgb, approximate=False)
            h = y * (jnp.einsum('bsd,fd->bsf', x, w1w) + w1b)
            out = jnp.einsum('bsf,df->bsd', h, w2w) + w2b
            return (acc + out * g[..., None], None)
        acc0 = jnp.zeros_like(x)
        out, _ = jax.lax.scan(body, acc0, (w1_w, w1_b, w2_w, w2_b, wg_w, wg_b, gates_e))
        return out
    x = x + _L0_xattn_ref(_layernorm(x, axis=-1), ctx_1024, ctx_1024, L0_xattn_wqg, L0_xattn_bqg, L0_xattn_wkg, L0_xattn_bkg, L0_xattn_wvg, L0_xattn_bvg, L0_xattn_wql, L0_xattn_bql, L0_xattn_wkl, L0_xattn_bkl, L0_xattn_wvl, L0_xattn_bvl, L0_xattn_wp, L0_xattn_bp)
    x = x + _L0_ffn_ref(_layernorm(x, axis=-1), L0_ffn_router_w, L0_ffn_w1_w, L0_ffn_w1_b, L0_ffn_w2_w, L0_ffn_w2_b, L0_ffn_wg_w, L0_ffn_wg_b)
    return x

_drawn_inputs = setup_inputs


def setup_inputs(seed=0):
    import zlib

    import numpy as np

    out = dict(_drawn_inputs(seed))
    spreads = {}
    factors = {'L0_ffn_router_w': 8.0,
     'L0_ffn_w1_w': 8.0,
     'L0_ffn_w1_b': 8.0,
     'L0_ffn_w2_w': 8.0,
     'L0_ffn_w2_b': 29.696,
     'L0_ffn_wg_w': 8.0,
     'L0_ffn_wg_b': 8.0}
    for name, (base, spread) in spreads.items():
        noise = np.random.default_rng([zlib.crc32(name.encode()), seed]).standard_normal(out[name].shape)
        drawn = base * np.exp(spread * noise) if base else spread * noise
        out[name] = jnp.asarray(drawn.astype(out[name].dtype))
    for name, factor in factors.items():
        out[name] = (out[name] * factor).astype(out[name].dtype)
    return out
```

```python
from contextlib import ExitStack

import concourse.bass as bass
from concourse import mybir

F32 = mybir.dt.float32
F32R = mybir.dt.float32r
BF16 = mybir.dt.bfloat16
F16 = mybir.dt.float16
I32 = mybir.dt.int32
ALU = mybir.AluOpType
ACT = mybir.ActivationFunctionType
AX = mybir.AxisListType.X

P = 128
B = 8
D = 128
H = 4
HD = D // H
E = 8
F = 512
FC = F // P
K = 2
W3 = 2 * F + FC * D
BW = 2 * F + D
PAIRS = K * B * P
T = (PAIRS + E * (P - 1)) // P
SCALE = float(D) ** -0.5
EPS = 1e-5
RAW = 3
PARTS = 3


def program(nc, x, ctxn, ctxT, cols, rows, bp_row, rwT, wpack, bias, out):
    with ExitStack() as st:
        def sb(name, shape, dt=F32):
            return st.enter_context(nc.sbuf_tensor(name, shape, dt))

        def sem(name):
            return st.enter_context(nc.semaphore(name))

        def dram(name, shape, dt=F32):
            return nc.dram_tensor(name, shape, dt, kind="Internal").ap()

        tokens_dram = dram("tokens_dram", [P * B, D])
        results_dram = dram("results_dram", [PAIRS + T * P, D])
        parts_dram = dram("parts_dram", [PARTS, E * BW], BF16)

        ident = sb("ident", [P, P])
        ones = sb("ones", [P, P])
        ones_bf = sb("ones_bf", [P, P], BF16)
        before = sb("before", [P, P], BF16)
        lower = sb("lower", [P, E, E])
        tile_edge = sb("tile_edge", [P, B])
        tile_no = sb("tile_no", [P, T])
        lane_no = sb("lane_no", [P, P], F16)
        src_id = sb("src_id", [P, K, B])
        dst_id = sb("dst_id", [P, K, B])
        pad_row = sb("pad_row", [P, T])
        pick = sb("pick", [P, E, P], BF16)
        minus_half = sb("minus_half", [P, B])

        xs = sb("xs", [P, B, D])
        cc = sb("cc", [P, 2, B, D])
        cn, cT = cc[:, 0], cc[:, 1]
        col = sb("col", [D, 5])
        row = sb("row", [D, 4, 2, HD])
        bp = sb("bp", [P, D])
        rw = sb("rw", [D, E])
        xn = sb("xn", [P, B, D])
        x1 = sb("x1", [P, B, D])
        stats = sb("stats", [P, B, 6])
        mean = sb("mean", [P, B])
        half = sb("half", [P, B])
        var = sb("var", [P, B])
        rstd = sb("rstd", [P, B])
        wqk = sb("wqk", [D, 2, HD])
        wqb = sb("wqb", [D, 2, HD])
        bqk = sb("bqk", [D, 2, HD])
        bqb = sb("bqb", [D, 2, HD])
        csum = sb("csum", [D, B, HD])
        gsel = sb("gsel", [D, B, HD])
        xsum = sb("xsum", [D, B])
        uq = sb("uq", [D, 2, B, HD])
        t2 = sb("t2", [D, 2, B, HD])
        s = sb("s", [D, 2, B, HD])
        smax = sb("smax", [D, 2 * B])
        rsum = sb("rsum", [D, 2 * B])
        mv = sb("mv", [D, 2, B, HD])
        mr = sb("mr", [D, 2, B, HD])
        mrT = sb("mrT", [D, 2, B, HD])
        blk = sb("blk", [D, 2, B, D])
        xn2 = sb("xn2", [P, B, D])
        xn2T = xs

        prob = sb("prob", [P, B, E])
        lmax = sb("lmax", [P, B])
        over, tie = (a[:].rearrange("p g b j -> p (g b j)").rearrange("p (b e f) -> p b e f", b=B, e=E)
                     for a in (uq, t2))
        rank = sb("rank", [P, B, E])
        chosen = sb("chosen", [P, B + 1, E], BF16)
        mask = sb("mask", [P, K, B, E])
        prod = sb("prod", [P, K, B, E])
        gate = sb("gate", [P, K, B])
        slot = sb("slot", [P, K, B])
        slot_i = sb("slot_i", [P, K * B], I32)
        tile_i = sb("tile_i", [P, K * B], I32)
        lane_i = sb("lane_i", [P, K * B], I32)
        lane = sb("lane", [P, K * B])
        place = sb("place", [P, B, E])
        cmp = sb("cmp", [P, E, B])
        ntile = sb("ntile", [P, E])
        first = sb("first", [P, E])
        past = sb("past", [P, E])
        cmp_t = sb("cmp_t", [P, T, E])
        expert = sb("expert", [P, T])
        expert_i = sb("expert_i", [P, T + 1], I32)
        in_tile = sb("in_tile", [P, K * B, T])
        tile_rhs = sb("tile_rhs", [P, K * B, 3, T], F16)
        lane_lhs = sb("lane_lhs", [P, K * B, P], F16)
        pad = sb("pad", [P, T])
        src_i = sb("src_i", [P, T], I32)
        dst_i = sb("dst_i", [P, T], I32)

        raw = sb("raw", [P, RAW, W3])
        w_hi = sb("w_hi", [P, E, W3], F32R)
        w_lo = sb("w_lo", [P, E, W3], F32R)
        b_raw = sb("b_raw", [P, E * BW // P])
        b_part = sb("b_part", [P, PARTS, E * BW // P], BF16)
        b_rest = sb("b_rest", [P, PARTS - 1, E * BW // P])
        b_rows = sb("b_rows", [P, BW], BF16)
        xg = sb("xg", [P, 2, D])
        xT_hi = sb("xT_hi", [D, 2, P], F32R)
        xT_lo = sb("xT_lo", [D, 2, P], F32R)
        act = sb("act", [P, 2, F])
        hid = sb("hid", [P, 2, F])
        hT_hi = sb("hT_hi", [P, 2, FC, P], F32R)
        hT_lo = sb("hT_lo", [P, 2, FC, P], F32R)
        y = sb("y", [P, 2, D])
        res = cc[:].rearrange("p k b d -> p (k b d)").rearrange("p (b k d) -> p b k d", b=B, k=K)
        fin = xn

        ps = st.enter_context(nc.psum_tensor("ps", [P, 8, 512], F32))
        G = ps[:, 0:2, :].rearrange("p k (b d) -> p (k b) d", d=D)
        XSUM = ps[:, 2, 0:B]
        CSUM = ps[:, 3:5, :].rearrange("p k (b d) -> p (k b) d", d=D)
        ATT = ps[:, 5:7, :].rearrange("p k (b d) -> p (k b) d", d=D)
        XN2T = G
        LOGIT = ps[:, 2, 64:64 + B * E].rearrange("p (b e) -> p b e", e=E)
        PLACE = ps[:, 3, 0:(B + 1) * E].rearrange("p (b e) -> p b e", e=E)
        INV = ps[:, 4, 0:3 * T].rearrange("p (c t) -> p c t", t=T)
        pG = [ps[:, 0, :], ps[:, 1, :]]
        pU = [ps[:, 2, :], ps[:, 3, :]]
        pH = [ps[:, 4, :].rearrange("p (c n) -> p c n", n=P), ps[:, 5, :].rearrange("p (c n) -> p c n", n=P)]
        pX = ps[:, 6, 0:P]
        pY = ps[:, 7, 0:D]

        x_in = sem("x_in"); c_in = sem("c_in"); cT_in = sem("cT_in"); small_in = sem("small_in")
        b_in = sem("b_in"); b_out = sem("b_out"); brow_in = sem("brow_in"); brow_zero = sem("brow_zero")
        raw_in = [sem(f"raw_in{i}") for i in range(RAW)]
        w_hi_done = sem("w_hi_done"); w_lo_done = sem("w_lo_done")
        b_split = sem("b_split")
        pool_step = sem("pool_step"); dve_step = sem("dve_step")
        consts = sem("consts"); blk_zero = sem("blk_zero")
        factors = sem("factors"); csum_ps = sem("csum_ps"); csum_sb = sem("csum_sb")
        uq_done = sem("uq_done"); xbp_done = sem("xbp_done")
        var_done = sem("var_done"); rstd_done = sem("rstd_done"); xn_done = sem("xn_done")
        g_ps = sem("g_ps"); g_act = sem("g_act"); xsum_sb = sem("xsum_sb"); t2_done = sem("t2_done")
        s_done = sem("s_done"); exp_done = sem("exp_done"); attn_done = sem("attn_done")
        r_done = sem("r_done"); mrT_done = sem("mrT_done"); blk_act = sem("blk_act"); blk_dve = sem("blk_dve")
        att_ps = sem("att_ps"); xn2_done = sem("xn2_done"); tokens_out = sem("tokens_out")
        xn2T_ps = sem("xn2T_ps"); xn2T_sb = sem("xn2T_sb"); logit_ps = sem("logit_ps")
        logit_sb = sem("logit_sb"); pexp_done = sem("pexp_done")
        chosen_done = sem("chosen_done"); place_ps = sem("place_ps"); experts_done = sem("experts_done")
        tile_rhs_done = sem("tile_rhs_done"); lane_lhs_done = sem("lane_lhs_done")
        inv_ps = sem("inv_ps"); index_done = sem("index_done")
        gathered = [sem("gathered0"), sem("gathered1")]
        scattered = [sem("scattered0"), sem("scattered1")]
        xT_ps = sem("xT_ps"); xT_hi_done = sem("xT_hi_done"); xT_lo_done = sem("xT_lo_done")
        gate_ps = sem("gate_ps"); up_ps = sem("up_ps"); act_done = sem("act_done"); hid_done = sem("hid_done")
        hT_ps = sem("hT_ps"); hT_hi_done = sem("hT_hi_done"); hT_lo_done = sem("hT_lo_done")
        y_ps = sem("y_ps"); y_done = sem("y_done")
        res_in = sem("res_in"); fin_done = sem("fin_done"); out_done = sem("out_done")

        N_SMALL = (4 + H) * 16
        N_CONST = 14

        def real(t):
            return not isinstance(t, int) or 0 <= t < T

        def again(t):
            return not isinstance(t, int) or t >= 2

        def pipeline(eng, turn):
            for s in range(-1, 4):
                turn(s, s % 2)
            with eng.Fori(4, T - 2, 2) as s:
                turn(s, 0)
                turn(s + 1, 1)
            for s in range(T - 1, T + 2):
                turn(s, s % 2)

        block = st.enter_context(nc.Block())

        @block.sync
        def _(sp):
            sp.dma_start(xs[:], x.rearrange("b n d -> n b d")).then_inc(x_in, 16)
            sp.dma_start(cn, ctxn.rearrange("b n d -> n b d")).then_inc(c_in, 16)
            for h in range(H):
                sp.dma_start(row[h * HD:(h + 1) * HD].rearrange("p a g j -> p (a g j)"),
                             rows[h:h + 1, :].to_broadcast([HD, 8 * HD])).then_inc(small_in, 16)
            sp.dma_start(col[:], cols).then_inc(small_in, 16)
            sp.dma_start(bp[:], bp_row.to_broadcast([P, D])).then_inc(small_in, 16)
            sp.dma_start(rw[:], rwT).then_inc(small_in, 16)
            sp.dma_start(cT, ctxT).then_inc(cT_in, 16)
            sp.dma_start(b_raw[:], bias).then_inc(small_in, 16)
            for e in range(E):
                if e >= RAW:
                    sp.wait_ge(w_lo_done, e - RAW + 1)
                sp.dma_start(raw[:, e % RAW, :], wpack[:, e, :]).then_inc(raw_in[e % RAW], 16)
                if e == 0:
                    sp.wait_ge(b_split, 1)
                    sp.dma_start(parts_dram.rearrange("j (p c) -> p j c", p=P), b_part[:]).then_inc(b_out, 16)
                    sp.wait_ge(b_out, 16)
                    sp.wait_ge(brow_zero, 1)
                    sp.dma_start(b_rows[0:PARTS * E, :], parts_dram.rearrange("j (e c) -> (j e) c", e=E)).then_inc(brow_in, 16)
            sp.wait_ge(xn2_done, 1)
            sp.dma_start(tokens_dram.rearrange("(n b) d -> n b d", b=B), xn2[:]).then_inc(tokens_out, 16)
            sp.wait_ge(scattered[0], 16 * ((T + 1) // 2))
            sp.wait_ge(scattered[1], 16 * (T // 2))
            sp.dma_start(res, results_dram[0:PAIRS, :].rearrange("(n b k) d -> n b k d", b=B, k=K)).then_inc(res_in, 16)
            for i in range(2):
                sp.wait_ge(fin_done, i + 1)
                bs = slice(i * B // 2, (i + 1) * B // 2)
                sp.dma_start(out[bs].rearrange("b n d -> n b d"), fin[:, bs, :]).then_inc(out_done, 16)
            sp.wait_ge(out_done, 32)

        @block.gpsimd
        def _(pool):
            done = [0]

            def step(ins):
                done[0] += 1
                ins.then_inc(pool_step, 1)
                pool.wait_ge(pool_step, done[0])

            step(pool.memset(minus_half[:], -0.5))
            step(pool.memset(b_rows[:], 0.0))
            pool.memset(before[:], 1.0).then_inc(brow_zero, 1)
            step(pool.memset(ident[:], 0.0))
            step(pool.memset(lower[:], 1.0))
            step(pool.memset(pick[:], 0.0))
            pool.affine_select(out=ident[:], in_=ident[:], compare_op=ALU.not_equal, fill=1.0, base=0,
                               pattern=[[-1, P]], channel_multiplier=1).then_inc(consts, 1)
            pool.memset(ones[:], 1.0).then_inc(consts, 1)
            pool.memset(ones_bf[:], 1.0).then_inc(consts, 1)
            pool.wait_ge(brow_zero, 1)
            pool.affine_select(out=before[:], in_=before[:], compare_op=ALU.is_gt, fill=0.0, base=0,
                               pattern=[[1, P]], channel_multiplier=-1).then_inc(consts, 1)
            pool.affine_select(out=lower[:], in_=lower[:], compare_op=ALU.is_gt, fill=0.0, base=0,
                               pattern=[[1, E], [-1, E]], channel_multiplier=0).then_inc(consts, 1)
            pool.iota(tile_edge[:], [[P, B]], base=0, channel_multiplier=0,
                      allow_small_or_imprecise_dtypes=True).then_inc(consts, 1)
            pool.iota(tile_no[:], [[1, T]], base=0, channel_multiplier=0,
                      allow_small_or_imprecise_dtypes=True).then_inc(consts, 1)
            pool.iota(lane_no[:], [[1, P]], base=0, channel_multiplier=0,
                      allow_small_or_imprecise_dtypes=True).then_inc(consts, 1)
            pool.iota(src_id[:], [[0, K], [1, B]], base=0, channel_multiplier=B,
                      allow_small_or_imprecise_dtypes=True).then_inc(consts, 1)
            pool.iota(dst_id[:], [[1, K], [K, B]], base=0, channel_multiplier=K * B,
                      allow_small_or_imprecise_dtypes=True).then_inc(consts, 1)
            pool.iota(pad_row[:], [[P, T]], base=PAIRS, channel_multiplier=1,
                      allow_small_or_imprecise_dtypes=True).then_inc(consts, 1)
            pool.memset(chosen[:, B, :], 0.0).then_inc(consts, 1)
            for j in range(PARTS):
                ins = pool.affine_select(out=pick[:], in_=pick[:], compare_op=ALU.not_equal, fill=1.0,
                                         base=-j * E, pattern=[[-1, E], [0, P]], channel_multiplier=1)
                if j < PARTS - 1:
                    step(ins)
                else:
                    ins.then_inc(consts, 1)
            pool.memset(blk[:], 0.0).then_inc(blk_zero, 1)
            pool.memset(expert_i[:, T:T + 1], 0).then_inc(consts, 1)

            pool.wait_ge(x_in, 16)
            pool.wait_ge(small_in, N_SMALL)
            pool.tensor_tensor(x1[:], xs[:], bp[:].unsqueeze(1).to_broadcast([P, B, D]), ALU.add).then_inc(xbp_done, 1)
            pool.wait_ge(var_done, 1)
            pool.tensor_tensor(rstd[:], var[:], minus_half[:], ALU.pow).then_inc(rstd_done, 1)
            pool.wait_ge(factors, 4)
            pool.wait_ge(csum_sb, 4)
            step(pool.tensor_tensor(uq[:], csum[:].unsqueeze(1).to_broadcast([D, 2, B, HD]),
                                    bqk[:].unsqueeze(2).to_broadcast([D, 2, B, HD]), ALU.mult))
            pool.tensor_tensor(uq[:], uq[:], bqb[:].unsqueeze(2).to_broadcast([D, 2, B, HD]), ALU.add).then_inc(uq_done, 1)
            pool.wait_ge(xsum_sb, 1)
            pool.tensor_tensor(t2[:], xsum[:].unsqueeze(1).unsqueeze(3).to_broadcast([D, 2, B, HD]),
                               wqb[:].unsqueeze(2).to_broadcast([D, 2, B, HD]), ALU.mult).then_inc(t2_done, 1)

            def low(e):
                pool.wait_ge(w_hi_done, e + 1)
                pool.tensor_tensor(w_lo[:, e, :], raw[:, e % RAW, :], w_hi[:, e, :].bitcast(F32),
                                   ALU.subtract).then_inc(w_lo_done, 1)

            low(0)
            pool.wait_ge(attn_done, 1)
            step(pool.tensor_tensor(t2[:], s[:], row[:, 3].unsqueeze(2).to_broadcast([D, 2, B, HD]), ALU.mult))
            pool.tensor_tensor(mr[:, 1], t2[:, 0], t2[:, 1], ALU.add).then_inc(r_done, 1)
            low(1)
            pool.wait_ge(var_done, 2)
            pool.tensor_tensor(rstd[:], var[:], minus_half[:], ALU.pow).then_inc(rstd_done, 1)
            for e in range(2, E):
                low(e)

            def gather(t):
                pool.indirect_dma_start(xg[:, t % 2, :], None, tokens_dram,
                                        bass.IndirectOffsetOnAxis(ap=src_i[:, t:t + 1], axis=0)).then_inc(gathered[t % 2], 16)

            def scatter(t):
                pool.wait_ge(y_done, t + 1)
                pool.indirect_dma_start(results_dram, bass.IndirectOffsetOnAxis(ap=dst_i[:, t:t + 1], axis=0),
                                        y[:, t % 2, :], None).then_inc(scattered[t % 2], 16)

            pool.wait_ge(index_done, 2)
            pool.wait_ge(tokens_out, 16)
            gather(0)
            gather(1)
            for t in range(T + 3):
                if t + 2 < T:
                    pool.wait_ge(xT_ps, t + 1)
                    gather(t + 2)
                if t >= 3:
                    scatter(t - 3)

        @block.scalar
        def _(sc):
            def high(e):
                sc.wait_ge(raw_in[e % RAW], 16 * (e // RAW + 1))
                sc.copy(w_hi[:, e, :], raw[:, e % RAW, :]).then_inc(w_hi_done, 1)

            sc.wait_ge(csum_ps, 2)
            for h in range(H):
                hs = slice(h * HD, (h + 1) * HD)
                sc.copy(csum[hs], CSUM[hs, :, hs]).then_inc(csum_sb, 1)
            high(0)
            sc.wait_ge(g_ps, B)
            for h in (2, 3):
                hs = slice(h * HD, (h + 1) * HD)
                sc.copy(gsel[hs], G[hs, :, hs]).then_inc(g_act, 1)
            high(1)
            sc.wait_ge(s_done, 1)
            sc.activation(s[:], s[:], ACT.Exp, scale=SCALE).then_inc(exp_done, 1)
            high(2)
            sc.wait_ge(mrT_done, 1)
            sc.wait_ge(blk_zero, 1)
            for h in (2, 3):
                hs = slice(h * HD, (h + 1) * HD)
                sc.copy(blk[hs, :, :, hs].rearrange("p m b d -> p (m b) d"),
                        mrT[hs].rearrange("p m b d -> p (m b) d")).then_inc(blk_act, 1)
            high(3)
            for i in range(2):
                sc.wait_ge(xn2T_ps, B // 2 * (i + 1))
                bs = slice(i * B // 2, (i + 1) * B // 2)
                sc.copy(xn2T[:, bs, :], XN2T[:, bs, :]).then_inc(xn2T_sb, 1)
            sc.wait_ge(logit_sb, 1)
            sc.activation(prob[:], prob[:], ACT.Exp).then_inc(pexp_done, 1)
            for e in range(4, E):
                high(e)

            def turn(s, q):
                if real(s + 1):
                    sc.wait_ge(xT_ps, s + 2)
                    if again(s + 1):
                        sc.wait_ge(up_ps, s)
                    sc.copy(xT_hi[:, 1 - q, :], pX).then_inc(xT_hi_done, 1)
                if real(s):
                    sc.wait_ge(gate_ps, s + 1)
                    if again(s):
                        sc.wait_ge(hid_done, s - 1)
                    sc.activation(act[:, q, :], pG[q], ACT.Gelu).then_inc(act_done, 1)
                if real(s - 1):
                    sc.wait_ge(hT_ps, s)
                    if again(s - 1):
                        sc.wait_ge(y_ps, s - 2)
                    sc.copy(hT_hi[:, 1 - q], pH[1 - q]).then_inc(hT_hi_done, 1)

            pipeline(sc, turn)

        @block.vector
        def _(v):
            done = [0]

            def step(ins):
                done[0] += 1
                ins.then_inc(dve_step, 1)
                v.wait_ge(dve_step, done[0])

            def mark(ins):
                done[0] += 1
                ins.then_inc(dve_step, 1)
                return done[0]

            def norm(src, dst, n, dst_done):
                for b in range(B):
                    k = mark(v.bn_stats(stats[:, b, :], src[:, b, :]))
                v.wait_ge(dve_step, k)
                mark(v.tensor_tensor(mean[:], stats[:, :, 1], stats[:, :, 4], ALU.add))
                mark(v.tensor_tensor(half[:], stats[:, :, 1], stats[:, :, 4], ALU.subtract))
                step(v.tensor_tensor(var[:], stats[:, :, 2], stats[:, :, 5], ALU.add))
                step(v.scalar_tensor_tensor(out=half[:], in0=half[:], scalar=D / 4.0, in1=half[:], op0=ALU.mult, op1=ALU.mult))
                step(v.tensor_tensor(var[:], var[:], half[:], ALU.add))
                v.tensor_scalar(var[:], var[:], 1.0 / D, EPS, ALU.mult, ALU.add).then_inc(var_done, 1)
                step(v.tensor_scalar(mean[:], mean[:], 0.5, None, ALU.mult))
                v.wait_ge(rstd_done, n)
                for b in range(B):
                    v.tensor_scalar(dst[:, b, :], src[:, b, :], mean[:, b:b + 1], rstd[:, b:b + 1],
                                    ALU.subtract, ALU.mult).then_inc(dst_done, 1)

            def by_head(a):
                return a.unsqueeze(2).to_broadcast([D, 2, B, HD])

            v.wait_ge(x_in, 16)
            norm(xs, xn, 1, xn_done)
            v.wait_ge(small_in, N_SMALL)
            for dst, a, c, f in ((wqk, 0, 0, 1.0), (wqb, 1, 0, 1.0), (bqk, 0, 2, 1.0), (bqb, 1, 2, float(P))):
                for g in range(2):
                    ins = v.tensor_scalar(dst[:, g, :], row[:, a, g, :], col[:, c + g:c + g + 1], f, ALU.mult, ALU.mult)
                ins.then_inc(factors, 1)
            step(v.tensor_copy(b_part[:, 0], b_raw[:]))
            step(v.tensor_tensor(b_rest[:, 0], b_raw[:], b_part[:, 0], ALU.subtract))
            step(v.tensor_copy(b_part[:, 1], b_rest[:, 0]))
            step(v.tensor_tensor(b_rest[:, 1], b_rest[:, 0], b_part[:, 1], ALU.subtract))
            v.tensor_copy(b_part[:, 2], b_rest[:, 1]).then_inc(b_split, 1)

            v.wait_ge(g_ps, B)
            v.tensor_copy(xsum[:], XSUM).then_inc(xsum_sb, 1)
            for h in (0, 1):
                hs = slice(h * HD, (h + 1) * HD)
                k = mark(v.tensor_copy(gsel[hs], G[hs, :, hs]))
            v.wait_ge(dve_step, k)
            v.wait_ge(g_act, 2)
            v.wait_ge(factors, 4)
            step(v.tensor_tensor(s[:], gsel[:].unsqueeze(1).to_broadcast([D, 2, B, HD]), by_head(wqk[:]), ALU.mult))
            v.wait_ge(uq_done, 1)
            step(v.tensor_tensor(s[:], s[:], uq[:], ALU.add))
            v.wait_ge(t2_done, 1)
            step(v.tensor_tensor(s[:], s[:], t2[:], ALU.add))
            s3 = s[:].rearrange("p g b j -> p (g b) j")
            step(v.tensor_reduce(smax[:], s3, AX, ALU.max))
            v.tensor_tensor(s3, s3, smax[:].unsqueeze(2).to_broadcast([D, 2 * B, HD]), ALU.subtract).then_inc(s_done, 1)
            v.wait_ge(exp_done, 1)
            step(v.tensor_reduce(rsum[:], s3, AX, ALU.add))
            step(v.reciprocal(rsum[:], rsum[:]))
            step(v.tensor_scalar(rsum[:], rsum[:], col[:, 4:5], 2.0, ALU.mult, ALU.mult))
            v.tensor_tensor(s3, s3, rsum[:].unsqueeze(2).to_broadcast([D, 2 * B, HD]), ALU.mult).then_inc(attn_done, 1)
            v.wait_ge(attn_done, 1)
            step(v.tensor_tensor(mv[:], s[:], by_head(row[:, 2]), ALU.mult))
            step(v.tensor_tensor(mr[:, 0], mv[:, 0], mv[:, 1], ALU.add))
            v.wait_ge(r_done, 1)
            v.transpose(mrT[:].rearrange("p m b j -> p (m b j)"), mr[:].rearrange("p m b j -> p (m b j)")).then_inc(mrT_done, 1)
            v.wait_ge(mrT_done, 1)
            v.wait_ge(blk_zero, 1)
            for h in (0, 1):
                hs = slice(h * HD, (h + 1) * HD)
                v.tensor_copy(blk[hs, :, :, hs].rearrange("p m b d -> p (m b) d"),
                              mrT[hs].rearrange("p m b d -> p (m b) d")).then_inc(blk_dve, 1)
            v.wait_ge(xbp_done, 1)
            for i in range(2):
                v.wait_ge(att_ps, i + 1)
                bs = slice(i * B // 2, (i + 1) * B // 2)
                k = mark(v.tensor_tensor(x1[:, bs, :], x1[:, bs, :], ATT[:, bs, :], ALU.add))
            v.wait_ge(dve_step, k)
            norm(x1, xn2, 2, xn2_done)

            v.wait_ge(logit_ps, 1)
            step(v.tensor_reduce(lmax[:], LOGIT, AX, ALU.max))
            v.tensor_tensor(prob[:], LOGIT, lmax[:].unsqueeze(2).to_broadcast([P, B, E]), ALU.subtract).then_inc(logit_sb, 1)
            v.wait_ge(pexp_done, 1)
            step(v.tensor_reduce(lmax[:], prob[:], AX, ALU.add))
            step(v.reciprocal(lmax[:], lmax[:]))
            step(v.tensor_tensor(prob[:], prob[:], lmax[:].unsqueeze(2).to_broadcast([P, B, E]), ALU.mult))
            v.wait_ge(consts, N_CONST)
            other = prob[:].unsqueeze(2).to_broadcast([P, B, E, E])
            own = prob[:].unsqueeze(3).to_broadcast([P, B, E, E])
            mark(v.tensor_tensor(over, other, own, ALU.is_gt))
            step(v.tensor_tensor(tie, other, own, ALU.is_equal))
            step(v.tensor_tensor(tie, tie, lower[:].unsqueeze(1).to_broadcast([P, B, E, E]), ALU.mult))
            step(v.tensor_tensor(over, over, tie, ALU.add))
            step(v.tensor_reduce(rank[:], over, AX, ALU.add))
            v.tensor_scalar(chosen[:, 0:B, :], rank[:], K - 0.5, None, ALU.is_lt).then_inc(chosen_done, 1)
            for k in range(K):
                n = mark(v.tensor_scalar(mask[:, k], rank[:], float(k), None, ALU.is_equal))
            v.wait_ge(dve_step, n)
            step(v.tensor_tensor(prod[:], mask[:], prob[:].unsqueeze(1).to_broadcast([P, K, B, E]), ALU.mult))
            step(v.tensor_reduce(gate[:], prod[:], AX, ALU.add))
            v.wait_ge(place_ps, 1)
            step(v.tensor_tensor(cmp[:], PLACE[:, B, :].unsqueeze(2).to_broadcast([P, E, B]),
                                 tile_edge[:].unsqueeze(1).to_broadcast([P, E, B]), ALU.is_gt))
            step(v.tensor_reduce(ntile[:], cmp[:], AX, ALU.add))
            step(v.tensor_tensor(cmp[:], lower[:], ntile[:].unsqueeze(1).to_broadcast([P, E, E]), ALU.mult))
            step(v.tensor_reduce(first[:], cmp[:], AX, ALU.add))
            mark(v.tensor_tensor(past[:], first[:], ntile[:], ALU.add))
            step(v.tensor_scalar(first[:], first[:], float(P), None, ALU.mult))
            step(v.tensor_tensor(place[:], PLACE[:, 0:B, :], first[:].unsqueeze(1).to_broadcast([P, B, E]), ALU.add))
            step(v.tensor_tensor(prod[:], mask[:], place[:].unsqueeze(1).to_broadcast([P, K, B, E]), ALU.mult))
            step(v.tensor_reduce(slot[:], prod[:], AX, ALU.add))
            step(v.tensor_copy(slot_i[:], slot[:].rearrange("p k b -> p (k b)")))
            mark(v.tensor_scalar(tile_i[:], slot_i[:], 7, None, ALU.logical_shift_right))
            step(v.tensor_scalar(lane_i[:], slot_i[:], P - 1, None, ALU.bitwise_and))
            step(v.tensor_copy(lane[:], lane_i[:]))
            for m in range(K * B):
                v.tensor_scalar(lane_lhs[:, m, :], lane_no[:], lane[:, m:m + 1], None, ALU.is_equal).then_inc(lane_lhs_done, 1)
            step(v.tensor_tensor(in_tile[:], tile_i[:].unsqueeze(2).to_broadcast([P, K * B, T]),
                                 tile_no[:].unsqueeze(1).to_broadcast([P, K * B, T]), ALU.is_equal))
            for c, ids in enumerate((src_id, dst_id)):
                v.tensor_tensor(tile_rhs[:, :, c, :], in_tile[:],
                                ids[:].rearrange("p k b -> p (k b)").unsqueeze(2).to_broadcast([P, K * B, T]),
                                ALU.mult).then_inc(tile_rhs_done, 1)
            v.tensor_copy(tile_rhs[:, :, 2, :], in_tile[:]).then_inc(tile_rhs_done, 1)
            step(v.tensor_tensor(cmp_t[:], tile_no[:].unsqueeze(2).to_broadcast([P, T, E]),
                                 past[:].unsqueeze(1).to_broadcast([P, T, E]), ALU.is_ge))
            step(v.tensor_reduce(expert[:], cmp_t[:], AX, ALU.add))
            v.tensor_scalar(expert_i[:, 0:T], expert[:], E - 1.0, None, ALU.min).then_inc(experts_done, 1)
            v.wait_ge(inv_ps, 1)
            v.tensor_copy(src_i[:], INV[:, 0, :]).then_inc(index_done, 1)
            step(v.tensor_tensor(pad[:], INV[:, 2, :], pad_row[:], ALU.mult))
            step(v.tensor_tensor(pad[:], pad_row[:], pad[:], ALU.subtract))
            v.tensor_tensor(dst_i[:], INV[:, 1, :], pad[:], ALU.add).then_inc(index_done, 1)

            def turn(s, q):
                if real(s + 1):
                    v.wait_ge(xT_hi_done, s + 2)
                    if again(s + 1):
                        v.wait_ge(up_ps, s)
                    v.tensor_tensor(xT_lo[:, 1 - q, :], pX, xT_hi[:, 1 - q, :].bitcast(F32),
                                    ALU.subtract).then_inc(xT_lo_done, 1)
                if real(s):
                    v.wait_ge(up_ps, s + 1)
                    v.wait_ge(act_done, s + 1)
                    if again(s):
                        v.wait_ge(hT_ps, s - 1)
                    v.tensor_tensor(hid[:, q, :], pU[q], act[:, q, :], ALU.mult).then_inc(hid_done, 1)
                if real(s - 1):
                    v.wait_ge(hT_hi_done, s)
                    if again(s - 1):
                        v.wait_ge(y_ps, s - 2)
                    v.tensor_tensor(hT_lo[:, 1 - q], pH[1 - q], hT_hi[:, 1 - q].bitcast(F32),
                                    ALU.subtract).then_inc(hT_lo_done, 1)
                if real(s - 2):
                    v.wait_ge(y_ps, s - 1)
                    if again(s - 2):
                        v.wait_ge(scattered[q], (s - 2 - q) * 8)
                    v.tensor_copy(y[:, q, :], pY).then_inc(y_done, 1)

            pipeline(v, turn)

            v.wait_ge(res_in, 16)
            for i in range(2):
                bs = range(i * B // 2, (i + 1) * B // 2)
                for b in bs:
                    k = mark(v.scalar_tensor_tensor(out=fin[:, b, :], in0=res[:, b, 0, :], scalar=gate[:, 0, b:b + 1],
                                                    in1=x1[:, b, :], op0=ALU.mult, op1=ALU.add))
                v.wait_ge(dve_step, k)
                for b in bs:
                    ins = v.scalar_tensor_tensor(out=fin[:, b, :], in0=res[:, b, 1, :], scalar=gate[:, 1, b:b + 1],
                                                 in1=fin[:, b, :], op0=ALU.mult, op1=ALU.add)
                ins.then_inc(fin_done, 1)

        @block.tensor
        def _(pe):
            pe.wait_ge(consts, 3)
            pe.wait_ge(c_in, 16)
            for i in range(2):
                pe.matmul(ps[:, 3 + i, :], ones[:], cn[:, 4 * i:4 * i + 4, :].rearrange("p b d -> p (b d)"),
                          start=True, stop=True).then_inc(csum_ps, 1)
            for b in range(B):
                pe.wait_ge(xn_done, b + 1)
                pe.matmul(XSUM[:, b:b + 1], xn[:, b, :], ones[:, 0:1], start=True, stop=True)
                pe.matmul(G[:, b, :], xn[:, b, :], cn[:, b, :], start=True, stop=True).then_inc(g_ps, 1)
            pe.wait_ge(blk_dve, 2)
            pe.wait_ge(blk_act, 2)
            pe.wait_ge(cT_in, 16)
            for i in range(2):
                bs = slice(4 * i, 4 * i + 4)
                pe.matmul(ps[:, 5 + i, :], ones[:], blk[:, 1, bs, :].rearrange("p b d -> p (b d)"), start=True, stop=False)
                for b in range(4 * i, 4 * i + 4):
                    mm = pe.matmul(ATT[:, b, :], cT[:, b, :], blk[:, 0, b, :], start=False, stop=(b % 4 == 3))
                mm.then_inc(att_ps, 1)
            for b in range(B):
                pe.wait_ge(xn2_done, b + 1)
                pe.transpose(XN2T[:, b, :], xn2[:, b, :], ident[:]).then_inc(xn2T_ps, 1)
            for b in range(B):
                if b % 4 == 0:
                    pe.wait_ge(xn2T_sb, b // 4 + 1)
                mm = pe.matmul(LOGIT[:, b, :], xn2T[:, b, :], rw[:], start=True, stop=True)
            mm.then_inc(logit_ps, 1)
            pe.wait_ge(consts, N_CONST)
            pe.wait_ge(chosen_done, 1)
            pe.matmul(PLACE, before[:], chosen[:], start=True, stop=False)
            for b in range(B):
                mm = pe.matmul(PLACE[:, b + 1:B + 1, :], ones_bf[:],
                               chosen[:, b, :].unsqueeze(1).to_broadcast([P, B - b, E]), start=False, stop=(b == B - 1))
            mm.then_inc(place_ps, 1)
            pe.wait_ge(tile_rhs_done, 3)
            for m in range(K * B):
                pe.wait_ge(lane_lhs_done, m + 1)
                mm = pe.matmul(INV, lane_lhs[:, m, :], tile_rhs[:, m], start=(m == 0), stop=(m == K * B - 1))
            mm.then_inc(inv_ps, 1)

            pe.wait_ge(experts_done, 1)
            pe.wait_ge(brow_in, 16)
            pe.wait_ge(w_hi_done, E)
            pe.wait_ge(w_lo_done, E)

            def expert_of(t):
                return pe.value_load(expert_i[0:1, bass.ds(t, 1)], min_val=0, max_val=E - 1)

            def turn(s, q):
                if real(s + 1):
                    pe.wait_ge(gathered[1 - q], (s + q) * 8 + 16)
                    if again(s + 2):
                        pe.wait_ge(xT_lo_done, s + 1)
                    pe.transpose(pX, xg[:, 1 - q, :], ident[:]).then_inc(xT_ps, 1)
                if real(s):
                    e = expert_of(s)
                    pe.wait_ge(xT_hi_done, s + 1)
                    pe.wait_ge(xT_lo_done, s + 1)
                    for c0, psum, used, ready in ((0, pG[q], act_done, gate_ps), (F, pU[q], hid_done, up_ps)):
                        if again(s):
                            pe.wait_ge(used, s - 1)
                        pe.matmul(psum, pick[:, e, :], b_rows[:, c0:c0 + F], start=True, stop=False)
                        pe.matmul(psum, xT_hi[:, q, :], w_lo[:, e, c0:c0 + F], start=False, stop=False)
                        pe.matmul(psum, xT_hi[:, q, :], w_hi[:, e, c0:c0 + F], start=False, stop=False)
                        pe.matmul(psum, xT_lo[:, q, :], w_hi[:, e, c0:c0 + F], start=False, stop=True).then_inc(ready, 1)
                if real(s - 1):
                    pe.wait_ge(hid_done, s)
                    if again(s - 1):
                        pe.wait_ge(hT_hi_done, s - 2)
                        pe.wait_ge(hT_lo_done, s - 2)
                    for c in range(FC):
                        mm = pe.transpose(pH[1 - q][:, c, :], hid[:, 1 - q, c * P:(c + 1) * P], ident[:])
                    mm.then_inc(hT_ps, 1)
                if real(s - 2):
                    e = expert_of(s - 2)
                    pe.wait_ge(hT_hi_done, s - 1)
                    pe.wait_ge(hT_lo_done, s - 1)
                    if again(s - 1):
                        pe.wait_ge(y_done, s - 2)
                    pe.matmul(pY, pick[:, e, :], b_rows[:, 2 * F:BW], start=True, stop=False)
                    for c in range(FC):
                        c0 = 2 * F + c * D
                        pe.matmul(pY, hT_hi[:, q, c, :], w_lo[:, e, c0:c0 + D], start=False, stop=False)
                        pe.matmul(pY, hT_hi[:, q, c, :], w_hi[:, e, c0:c0 + D], start=False, stop=False)
                        mm = pe.matmul(pY, hT_lo[:, q, c, :], w_hi[:, e, c0:c0 + D], start=False, stop=(c == FC - 1))
                    mm.then_inc(y_ps, 1)

            pipeline(pe, turn)


def kernel(**inputs):
    import numpy as np
    import concourse.bacc as bacc
    from concourse.bass_utils import run_bass_kernel_spmd as run

    a = {k.replace("L0_xattn_", "").replace("L0_ffn_", ""): np.asarray(v) for k, v in inputs.items()}
    cols = np.stack([a[k] for k in ("wqg", "wql", "bqg", "bql", "wp")], axis=1)
    rows = np.stack([a[k].reshape(H, HD) for k in ("wkg", "wkl", "bkg", "bkl", "wvg", "wvl", "bvg", "bvl")], axis=1)
    wpack = np.concatenate([
        a["wg_w"].transpose(2, 0, 1), a["w1_w"].transpose(2, 0, 1),
        a["w2_w"].reshape(E, D, FC, P).transpose(3, 0, 2, 1).reshape(P, E, FC * D)], axis=2)
    bias = np.concatenate([a["wg_b"], a["w1_b"], a["w2_b"]], axis=1)
    arrays = {
        "x": a["x"], "ctxn": a["ctx_1024"], "ctxT": a["ctx_1024"].transpose(2, 0, 1), "cols": cols,
        "rows": rows.reshape(H, 8 * HD), "bp_row": a["bp"].reshape(1, D), "rwT": a["router_w"].T,
        "wpack": wpack, "bias": bias.reshape(P, E * BW // P),
    }
    arrays = {k: np.ascontiguousarray(v) for k, v in arrays.items()}
    nc = bacc.Bacc("TRN2", target_bir_lowering=False, num_devices=1)
    args = [nc.dram_tensor(k, v.shape, F32, kind="ExternalInput").ap() for k, v in arrays.items()]
    out = nc.dram_tensor("out", (B, P, D), F32, kind="ExternalOutput").ap()
    program(nc, *args, out)
    r = run(nc, [arrays], core_ids=[0])
    return r.results[0]["out"]
```

```python
from contextlib import ExitStack

import concourse.bass as bass
from concourse import mybir

F32 = mybir.dt.float32
F32R = mybir.dt.float32r
BF16 = mybir.dt.bfloat16
F16 = mybir.dt.float16
I32 = mybir.dt.int32
ALU = mybir.AluOpType
ACT = mybir.ActivationFunctionType
AX = mybir.AxisListType.X

P = 128
B = 8
D = 128
H = 4
HD = D // H
E = 8
F = 512
FC = F // P
K = 2
W3 = 2 * F + FC * D
BW = 2 * F + D
SMALL = 8 * HD + 5 + E + E * BW // P
PAIRS = K * B * P
T = (PAIRS + E * (P - 1)) // P
SCALE = float(D) ** -0.5
EPS = 1e-5
XG = 4
GN = 2
GB = B // GN
PARTS = 3


def program(nc, x, ctxn, ctxT, small_pack, bp_row, wpack, out):
    with ExitStack() as st:
        def sb(name, shape, dt=F32):
            return st.enter_context(nc.sbuf_tensor(name, shape, dt))

        def sem(name):
            return st.enter_context(nc.semaphore(name))

        def dram(name, shape, dt=F32):
            return nc.dram_tensor(name, shape, dt, kind="Internal").ap()

        tokens_dram = dram("tokens_dram", [P * B, D])
        results_dram = dram("results_dram", [PAIRS + T * P, D])
        parts_dram = dram("parts_dram", [PARTS, E * BW], BF16)

        ident = sb("ident", [P, P])
        ones = sb("ones", [P, P])
        ones_bf = sb("ones_bf", [P, P], BF16)
        before = sb("before", [P, P], BF16)
        lower = sb("lower", [P, E, E])
        lower_p = sb("lower_p", [P, E, E])
        tile_edge = sb("tile_edge", [P, T])
        tile_no = sb("tile_no", [P, T])
        lane_no = sb("lane_no", [P, P], F16)
        src_id = sb("src_id", [P, K, B])
        pad_row = sb("pad_row", [P, T])
        rank_no = sb("rank_no", [P, E])
        row_no = sb("row_no", [P, 1], I32)
        pick = sb("pick", [P, E, P], BF16)
        minus_half = sb("minus_half", [P, B])

        xs = sb("xs", [P, B, D])
        CW = D + 1
        cc = sb("cc", [P, B * (CW + P)])
        cn = cc[:, 0:B * CW].rearrange("p (b d) -> p b d", d=CW)
        cT = cc[:, B * CW:].rearrange("p (b n) -> p b n", n=P)
        small = sb("small", [P, SMALL])
        row = small[:, 0:8 * HD].rearrange("p (a g j) -> p a g j", a=4, g=2)
        col = small[:, 8 * HD:8 * HD + 5]
        rw = small[:, 8 * HD + 5:8 * HD + 5 + E]
        b_raw = small[:, 8 * HD + 5 + E:SMALL]
        bp = sb("bp", [1, D])
        xn = sb("xn", [P, B, D])
        x1 = sb("x1", [P, B, D])
        stats = sb("stats", [P, B, 6])
        mean = sb("mean", [P, B])
        half = sb("half", [P, B])
        var = sb("var", [P, B])
        rstd = sb("rstd", [P, B])
        wqk = sb("wqk", [D, 2, HD])
        wqb = sb("wqb", [D, 2, HD])
        bqk = sb("bqk", [D, 2, HD])
        bqb = sb("bqb", [D, 2, HD])
        csum = sb("csum", [D, B, HD])
        gsel = sb("gsel", [D, B, HD])
        xsum = sb("xsum", [D, B])
        nmr = sb("nmr", [P, B])
        uq = sb("uq", [D, GN, 2, GB, HD])
        t2 = sb("t2", [D, GN, 2, GB, HD])
        s = sb("s", [D, GN, 2, GB, HD])
        smax = sb("smax", [D, GN, 2 * GB])
        rsum = sb("rsum", [D, GN, 2 * GB])
        mv = sb("mv", [D, GN, 2, GB, HD])
        mr = sb("mr", [D, GN, 2, GB, HD])
        mrT = sb("mrT", [D, GN, 2, GB, HD])
        blk = sb("blk", [D, GN, 2, GB, D])
        xn2 = sb("xn2", [P, B, D])
        xn2T = xs

        prob = sb("prob", [P, B, E])
        lmax = sb("lmax", [P, B])
        logit = sb("logit", [P, B, E])
        second = sb("second", [P, B, E])
        key = sb("key", [P, B, E])
        kmax = sb("kmax", [P, B])
        psum_e = sb("psum_e", [P, B])
        chosen = sb("chosen", [P, B + 1, E], BF16)
        mask = sb("mask", [P, K, B, E])
        prod = sb("prod", [P, K, B, E])
        gated = sb("gated", [P, K, B, E])
        gate = sb("gate", [P, K, B])
        slot_i = sb("slot_i", [P, K * B], I32)
        tile_i = sb("tile_i", [P, K * B], I32)
        lane_i = sb("lane_i", [P, K * B], I32)
        place = sb("place", [P, B, E])
        cmp = sb("cmp", [P, E, B])
        ntile = sb("ntile", [P, E])
        first = sb("first", [P, E])
        past = sb("past", [P, E])
        cmp_t = sb("cmp_t", [P, T, E])
        expert = sb("expert", [P, T])
        expert_i = sb("expert_i", [P, T + 1], I32)
        in_tile = sb("in_tile", [P, K * B, T])
        tile_rhs = sb("tile_rhs", [P, K * B, 2, T], F16)
        lane_lhs = sb("lane_lhs", [P, K * B, P], F16)
        src = sb("src", [P, T])
        dst = sb("dst", [P, T])
        pad = sb("pad", [P, T])
        src_i = sb("src_i", [P, T], I32)
        dst_i = sb("dst_i", [P, T], I32)

        w_hi = sb("w_hi", [P, E, 2 * F], F32R)
        w_lo = sb("w_lo", [P, E, 2 * F], F32R)
        w_down = sb("w_down", [P, E, FC, 2, D], F32R)
        b_part = sb("b_part", [P, PARTS, E * BW // P], BF16)
        b_rest = sb("b_rest", [P, PARTS - 1, E * BW // P])
        b_rows = sb("b_rows", [P, BW], BF16)
        xg = sb("xg", [P, XG, D])
        xT_hi = sb("xT_hi", [D, 2, P], F32R)
        xT_lo = sb("xT_lo", [D, 2, P], F32R)
        act = sb("act", [P, 2, F])
        hid = sb("hid", [P, 2, F])
        hT_hi = sb("hT_hi", [P, 2, FC, P], F32R)
        hT_lo = sb("hT_lo", [P, 2, FC, P], F32R)
        y = sb("y", [P, 2, D])
        res = cc[:, 0:B * K * D].rearrange("p (b k d) -> p b k d", b=B, k=K)
        fin = xn

        ps = st.enter_context(nc.psum_tensor("ps", [P, 8, 512], F32))
        G = [ps[:, 2 * g:2 * g + 2, 0:2 * CW].rearrange("p k (b d) -> p k b d", d=CW) for g in range(GN)]
        CSUM = ps[:, 4:6, :].rearrange("p k (b d) -> p (k b) d", d=D)
        ATT = [ps[:, 6 + g, :].rearrange("p (b d) -> p b d", d=D) for g in range(GN)]
        XN2T = [ps[:, g, :].rearrange("p (b d) -> p b d", d=D) for g in range(GN)]
        LOGIT = [ps[:, 2 + g, 0:GB * E].rearrange("p (b e) -> p b e", e=E) for g in range(GN)]
        PLACE = ps[:, 4, 0:(B + 1) * E].rearrange("p (b e) -> p b e", e=E)
        INV = ps[:, 5, 0:2 * T].rearrange("p (c t) -> p c t", t=T)
        pG = [ps[:, 0, :], ps[:, 1, :]]
        pU = [ps[:, 2, :], ps[:, 3, :]]
        pH = [ps[:, 4, :].rearrange("p (c n) -> p c n", n=P), ps[:, 5, :].rearrange("p (c n) -> p c n", n=P)]
        pX = ps[:, 6, 0:P]
        pY = ps[:, 7, 0:2 * D]

        x_in = [sem("x_in0"), sem("x_in1")]
        c_in = sem("c_in"); cT_in = sem("cT_in"); small_in = sem("small_in")
        b_out = sem("b_out"); brow_in = sem("brow_in"); brow_zero = sem("brow_zero")
        bp_in = sem("bp_in")
        w_in = [sem(f"w_in{e}") for e in range(E)]
        w_hi_done = sem("w_hi_done"); w_lo_pool = sem("w_lo_pool"); w_lo_dve = sem("w_lo_dve")
        b_split = sem("b_split")
        pool_step = sem("pool_step"); dve_step = sem("dve_step")
        consts = sem("consts"); ones_col = sem("ones_col"); blk_zero = sem("blk_zero"); pick_done = sem("pick_done")
        factors = sem("factors"); csum_ps = sem("csum_ps"); csum_sb = sem("csum_sb")
        uq_done = sem("uq_done")
        var_done = sem("var_done"); rstd_done = sem("rstd_done"); nmr_done = sem("nmr_done")
        xn_dve = sem("xn_dve"); xn_act = sem("xn_act")
        g_ps = sem("g_ps"); g_act = sem("g_act"); xsum_sb = sem("xsum_sb"); t2_done = sem("t2_done")
        s_done = sem("s_done"); exp_done = sem("exp_done"); attn_done = sem("attn_done")
        r_done = sem("r_done"); mrT_done = sem("mrT_done"); blk_act = sem("blk_act"); blk_dve = sem("blk_dve")
        att_ps = sem("att_ps"); xn2_dve = sem("xn2_dve"); xn2_act = sem("xn2_act"); tokens_out = sem("tokens_out")
        x1_done = sem("x1_done")
        xn2T_ps = sem("xn2T_ps"); xn2T_sb = sem("xn2T_sb"); logit_ps = sem("logit_ps")
        logit_sb = sem("logit_sb"); pexp_done = sem("pexp_done")
        chosen_done = sem("chosen_done"); place_ps = sem("place_ps"); experts_done = sem("experts_done")
        lane_done = sem("lane_done"); in_tile_done = sem("in_tile_done"); tile_rhs_act = sem("tile_rhs_act"); tile_rhs_done = sem("tile_rhs_done")
        lane_dve = sem("lane_dve"); lane_pool = sem("lane_pool")
        inv_ps = sem("inv_ps"); src_done = sem("src_done"); dst_done = sem("dst_done")
        gathered = [sem(f"gathered{i}") for i in range(XG)]
        scattered = [sem("scattered0"), sem("scattered1")]
        xT_ps = sem("xT_ps"); xT_hi_done = sem("xT_hi_done"); xT_lo_done = sem("xT_lo_done")
        gate_ps = sem("gate_ps"); up_ps = sem("up_ps"); act_done = sem("act_done"); hid_done = sem("hid_done")
        hT_ps = sem("hT_ps"); hT_hi_done = sem("hT_hi_done"); hT_lo_done = sem("hT_lo_done")
        y_ps = sem("y_ps"); y_done = sem("y_done")
        res_in = [sem(f"res_in{i}") for i in range(4)]
        fin_done = sem("fin_done"); out_done = sem("out_done")

        N_CONST = 10
        LANES_POOL = 3
        DVE_LOWS = (1, 3, 5, 7)

        def chunks(a):
            return a.rearrange("p (c d) -> p c d", d=D)

        def low_gate_up(eng, e):
            eng.wait_ge(w_hi_done, e + 1)
            return eng.tensor_tensor(w_lo[:, e, :], w_lo[:, e, :].bitcast(F32), w_hi[:, e, :].bitcast(F32), ALU.subtract)

        def low_down(eng, e):
            eng.wait_ge(w_hi_done, e + 1)
            return eng.tensor_tensor(w_down[:, e, :, 1, :], w_down[:, e, :, 1, :].bitcast(F32),
                                     w_down[:, e, :, 0, :].bitcast(F32), ALU.subtract)

        UNROLL = XG
        HEAD = 4
        TAIL = HEAD + (T - 1 - HEAD) // UNROLL * UNROLL

        def real(t):
            return not isinstance(t, int) or 0 <= t < T

        def again(t):
            return not isinstance(t, int) or t >= 2

        def pipeline(eng, turn):
            for s in range(-2, HEAD):
                turn(s, s % UNROLL, s % 2)
            with eng.Fori(HEAD, TAIL, UNROLL) as s:
                for i in range(UNROLL):
                    turn(s + i, i, i % 2)
            for s in range(TAIL, T + 2):
                turn(s, s % UNROLL, s % 2)

        block = st.enter_context(nc.Block())

        @block.sync
        def _(sp):
            sp.dma_start(xs[:, 0:GB, :], x[0:GB].rearrange("b n d -> n b d")).then_inc(x_in[0], 16)
            sp.dma_start(cn[:, :, 0:D], ctxn.rearrange("b n d -> n b d")).then_inc(c_in, 16)
            for e in range(E):
                sp.dma_start(w_lo[:, e, :].bitcast(F32), wpack[:, e, 0:2 * F]).then_inc(w_in[e], 16)
                sp.dma_start(w_down[:, e, :, 1, :].bitcast(F32), chunks(wpack[:, e, 2 * F:W3])).then_inc(w_in[e], 16)
                if e == 2:
                    sp.dma_start(cT, ctxT).then_inc(cT_in, 16)
            sp.wait_ge(b_split, 1)
            sp.dma_start(parts_dram.rearrange("j (p c) -> p j c", p=P), b_part[:]).then_inc(b_out, 16)
            sp.wait_ge(b_out, 16)
            sp.wait_ge(brow_zero, 1)
            sp.dma_start(b_rows[0:PARTS * E, :], parts_dram.rearrange("j (e c) -> (j e) c", e=E)).then_inc(brow_in, 16)
            tokens = tokens_dram.rearrange("(n b) d -> n b d", b=B)
            for g in range(GN):
                sp.wait_ge(xn2_dve, GB // 2 * (g + 1))
                sp.wait_ge(xn2_act, GB // 2 * (g + 1))
                gs = slice(g * GB, (g + 1) * GB)
                sp.dma_start(tokens[:, gs, :], xn2[:, gs, :]).then_inc(tokens_out, 16)
            sp.wait_ge(scattered[0], 16 * ((T + 1) // 2))
            sp.wait_ge(scattered[1], 16 * (T // 2))
            rows_of = results_dram[0:PAIRS, :].rearrange("(n b k) d -> n b k d", b=B, k=K)
            for i in range(0, 4, 2):
                sp.dma_start(res[:, 2 * i:2 * i + 2], rows_of[:, 2 * i:2 * i + 2]).then_inc(res_in[i], 16)
            for i in range(4):
                sp.wait_ge(fin_done, i + 1)
                sp.dma_start(out[2 * i:2 * i + 2].rearrange("b n d -> n b d"), fin[:, 2 * i:2 * i + 2, :]).then_inc(out_done, 16)
            sp.wait_ge(out_done, 64)

        @block.gpsimd
        def _(pool):
            done = [0]

            def step(ins):
                done[0] += 1
                ins.then_inc(pool_step, 1)
                pool.wait_ge(pool_step, done[0])

            def count(ap, pattern, base=0, per_row=0):
                pool.iota(ap, pattern, base=base, channel_multiplier=per_row,
                          allow_small_or_imprecise_dtypes=True).then_inc(consts, 1)

            pool.memset(ones[:], 1.0).then_inc(ones_col, 1)
            pool.memset(cn[:, :, D:CW], 1.0).then_inc(ones_col, 1)
            pool.memset(minus_half[:], -0.5)
            pool.memset(lower_p[:], float(P))
            pool.memset(before[:], 1.0)
            step(pool.memset(lower[:], 1.0))
            pool.affine_select(out=before[:], in_=before[:], compare_op=ALU.is_gt, fill=0.0, base=0,
                               pattern=[[1, P]], channel_multiplier=-1).then_inc(consts, 1)
            for a in (lower, lower_p):
                pool.affine_select(out=a[:], in_=a[:], compare_op=ALU.is_gt, fill=0.0, base=0,
                                   pattern=[[1, E], [-1, E]], channel_multiplier=0).then_inc(consts, 1)
            pool.iota(row_no[:], [[0, 1]], base=0, channel_multiplier=1).then_inc(ones_col, 1)
            pool.memset(ones_bf[:], 1.0).then_inc(ones_col, 1)
            count(tile_edge[:], [[P, T]])
            count(tile_no[:], [[1, T]])
            count(lane_no[:], [[1, P]])
            count(src_id[:], [[0, K], [1, B]], per_row=B)
            step(pool.memset(ident[:], 0.0))
            pool.affine_select(out=ident[:], in_=ident[:], compare_op=ALU.not_equal, fill=1.0, base=0,
                               pattern=[[-1, P]], channel_multiplier=1).then_inc(consts, 1)
            count(pad_row[:], [[P, T]], base=PAIRS + 1, per_row=1)
            count(rank_no[:], [[-1, E]], base=E)

            def low(e):
                low_gate_up(pool, e)
                low_down(pool, e).then_inc(w_lo_pool, 1)

            def inverse_root(n):
                g = n % GN
                pool.wait_ge(var_done, n + 1)
                gs = slice(g * GB, (g + 1) * GB)
                pool.tensor_tensor(rstd[:, gs], var[:, gs], minus_half[:, gs], ALU.pow).then_inc(rstd_done, 1)

            inverse_root(0)
            inverse_root(1)
            pool.wait_ge(factors, 2)
            pool.wait_ge(csum_sb, 4)
            for g in range(GN):
                cs = csum[:, g * GB:(g + 1) * GB].unsqueeze(1).to_broadcast([D, 2, GB, HD])
                step(pool.tensor_tensor(uq[:, g], cs, bqk[:].unsqueeze(2).to_broadcast([D, 2, GB, HD]), ALU.mult))
                pool.tensor_tensor(uq[:, g], uq[:, g], bqb[:].unsqueeze(2).to_broadcast([D, 2, GB, HD]),
                                   ALU.add).then_inc(uq_done, 1)
            for g in range(GN):
                pool.wait_ge(xsum_sb, g + 1)
                gs = slice(g * GB, (g + 1) * GB)
                pool.tensor_tensor(t2[:, g], xsum[:, gs].unsqueeze(1).unsqueeze(3).to_broadcast([D, 2, GB, HD]),
                                   wqb[:].unsqueeze(2).to_broadcast([D, 2, GB, HD]), ALU.mult).then_inc(t2_done, 1)
            for g in range(GN):
                pool.wait_ge(attn_done, g + 1)
                step(pool.tensor_tensor(t2[:, g], s[:, g], row[:, 3].unsqueeze(2).to_broadcast([D, 2, GB, HD]), ALU.mult))
                pool.tensor_tensor(mr[:, g, 1], t2[:, g, 0], t2[:, g, 1], ALU.add).then_inc(r_done, 1)
            low(0)
            low(2)
            inverse_root(2)
            inverse_root(3)
            low(4)
            low(6)
            pool.wait_ge(lane_done, 1)
            for m in range(K * B - LANES_POOL, K * B):
                pool.tensor_scalar(lane_lhs[:, m, :], lane_no[:], lane_i[:, m:m + 1], None, ALU.is_equal).then_inc(lane_pool, 1)

            def gather(t):
                if t >= XG:
                    pool.wait_ge(xT_ps, t + 1 - XG)
                pool.indirect_dma_start(xg[:, t % XG, :], None, tokens_dram,
                                        bass.IndirectOffsetOnAxis(ap=src_i[:, t:t + 1], axis=0)).then_inc(gathered[t % XG], 16)

            def scatter(t):
                pool.wait_ge(y_done, t + 1)
                pool.indirect_dma_start(results_dram, bass.IndirectOffsetOnAxis(ap=dst_i[:, t:t + 1], axis=0),
                                        y[:, t % 2, :], None).then_inc(scattered[t % 2], 16)

            pool.wait_ge(src_done, 1)
            pool.wait_ge(tokens_out, 32)
            for t in range(XG):
                gather(t)
            for t in range(T + 2):
                if t + XG < T:
                    gather(t + XG)
                if t == 2:
                    pool.wait_ge(dst_done, 1)
                if t >= 2:
                    scatter(t - 2)

        @block.scalar
        def _(sc):
            sc.dma_start(xs[:, GB:B, :], x[GB:B].rearrange("b n d -> n b d")).then_inc(x_in[1], 16)
            sc.dma_start(small[:], small_pack).then_inc(small_in, 16)
            sc.dma_start(bp[:], bp_row).then_inc(bp_in, 16)

            def high(e):
                sc.wait_ge(w_in[e], 32)
                sc.copy(w_hi[:, e, :], w_lo[:, e, :].bitcast(F32))
                sc.copy(w_down[:, e, :, 0, :], w_down[:, e, :, 1, :].bitcast(F32)).then_inc(w_hi_done, 1)

            def normed(src, dst, g, n, dst_done):
                sc.wait_ge(nmr_done, n + 1)
                for b in range(g * GB + 1, (g + 1) * GB, 2):
                    sc.activation(dst[:, b, :], src[:, b, :], ACT.Identity, bias=nmr[:, b:b + 1],
                                  scale=rstd[:, b:b + 1]).then_inc(dst_done, 1)

            for g in range(GN):
                normed(xs, xn, g, g, xn_act)
            sc.wait_ge(csum_ps, 2)
            for h in range(H):
                hs = slice(h * HD, (h + 1) * HD)
                sc.copy(csum[hs], CSUM[hs, :, hs]).then_inc(csum_sb, 1)
            high(0)
            for g in range(GN):
                sc.wait_ge(xsum_sb, g + 1)
                for h in (2, 3):
                    hs = slice(h * HD, (h + 1) * HD)
                    sc.copy(gsel[hs, g * GB:(g + 1) * GB].rearrange("p (k b) j -> p k b j", k=2),
                            G[g][hs, :, :, hs]).then_inc(g_act, 1)
            high(1)
            for g in range(GN):
                sc.wait_ge(s_done, g + 1)
                sc.activation(s[:, g], s[:, g], ACT.Exp, scale=SCALE).then_inc(exp_done, 1)
            high(2)
            for g in range(GN):
                sc.wait_ge(mrT_done, g + 1)
                sc.wait_ge(blk_zero, 1)
                for h in (2, 3):
                    hs = slice(h * HD, (h + 1) * HD)
                    sc.copy(blk[hs, g, :, :, hs].rearrange("p m b d -> p (m b) d"),
                            mrT[hs, g].rearrange("p m b d -> p (m b) d")).then_inc(blk_act, 1)
            for e in range(3, E):
                high(e)
            for g in range(GN):
                gs = slice(g * GB, (g + 1) * GB)
                normed(x1, xn2, g, GN + g, xn2_act)
                sc.wait_ge(xn2T_ps, GB * (g + 1))
                sc.copy(xn2T[:, gs, :], XN2T[g]).then_inc(xn2T_sb, 1)
            for g in range(GN):
                gs = slice(g * GB, (g + 1) * GB)
                sc.wait_ge(logit_sb, g + 1)
                sc.activation(prob[:, gs], logit[:, gs], ACT.Exp).then_inc(pexp_done, 1)
            sc.activation(act[:, 0, 0:1], minus_half[:, 0:1], ACT.Gelu)
            sc.wait_ge(in_tile_done, 1)
            for k in range(K):
                sc.mul(tile_rhs[:, k * B:(k + 1) * B, 1, :], in_tile[:, k * B:(k + 1) * B], k + 1.0).then_inc(tile_rhs_act, 1)

            def turn(s, i, q):
                if real(s):
                    sc.wait_ge(gate_ps, s + 1)
                    if again(s):
                        sc.wait_ge(hid_done, s - 1)
                    sc.activation(act[:, q, :], pG[q], ACT.Gelu).then_inc(act_done, 1)
                if real(s - 1):
                    sc.wait_ge(hT_ps, s)
                    if again(s - 1):
                        sc.wait_ge(y_ps, s - 2)
                    sc.copy(hT_hi[:, 1 - q], pH[1 - q]).then_inc(hT_hi_done, 1)
                if real(s + 2):
                    sc.wait_ge(xT_ps, s + 3)
                    if again(s + 2):
                        sc.wait_ge(up_ps, s + 1)
                    sc.copy(xT_hi[:, q, :], pX).then_inc(xT_hi_done, 1)

            pipeline(sc, turn)

            sc.wait_ge(scattered[0], 16 * ((T + 1) // 2))
            sc.wait_ge(scattered[1], 16 * (T // 2))
            rows_of = results_dram[0:PAIRS, :].rearrange("(n b k) d -> n b k d", b=B, k=K)
            for i in range(1, 4, 2):
                sc.dma_start(res[:, 2 * i:2 * i + 2], rows_of[:, 2 * i:2 * i + 2]).then_inc(res_in[i], 16)

        @block.vector
        def _(v):
            done = [0]

            def mark(ins):
                done[0] += 1
                ins.then_inc(dve_step, 1)
                return done[0]

            def after(n):
                v.wait_ge(dve_step, n)

            def step(ins):
                after(mark(ins))

            def both(op):
                for g in range(GN):
                    if last[g]:
                        after(last[g])
                    last[g] = mark(op(g))

            last = [0] * GN

            def part(a, g):
                return a[:, g * GB:(g + 1) * GB]

            def stats_of(src, g):
                for b in range(g * GB, (g + 1) * GB):
                    last[g] = mark(v.bn_stats(stats[:, b, :], src[:, b, :]))

            def variance(gs, n):
                st = [stats[:, g * GB:(g + 1) * GB, :] for g in range(GN)]
                for g in gs:
                    after(last[g])
                    mark(v.tensor_tensor(part(half, g), st[g][:, :, 1], st[g][:, :, 4], ALU.subtract))
                    mark(v.tensor_tensor(part(mean, g), st[g][:, :, 1], st[g][:, :, 4], ALU.add))
                    last[g] = mark(v.tensor_tensor(part(var, g), st[g][:, :, 2], st[g][:, :, 5], ALU.add))
                for g in gs:
                    after(last[g])
                    last[g] = mark(v.scalar_tensor_tensor(out=part(half, g), in0=part(half, g), scalar=D / 4.0,
                                                          in1=part(half, g), op0=ALU.mult, op1=ALU.mult))
                for g in gs:
                    after(last[g])
                    last[g] = mark(v.tensor_tensor(part(var, g), part(var, g), part(half, g), ALU.add))
                for g in gs:
                    after(last[g])
                    v.tensor_scalar(part(var, g), part(var, g), 1.0 / D, EPS, ALU.mult, ALU.add).then_inc(var_done, 1)
                    last[g] = mark(v.tensor_scalar(part(mean, g), part(mean, g), 0.5, None, ALU.mult))

            def normed(src, dst, g, n, dst_done):
                v.wait_ge(rstd_done, n + 1)
                after(last[g])
                v.scalar_tensor_tensor(out=part(nmr, g), in0=part(mean, g), scalar=-1.0, in1=part(rstd, g),
                                       op0=ALU.mult, op1=ALU.mult).then_inc(nmr_done, 1)
                for b in range(g * GB, (g + 1) * GB, 2):
                    v.tensor_scalar(dst[:, b, :], src[:, b, :], mean[:, b:b + 1], rstd[:, b:b + 1],
                                    ALU.subtract, ALU.mult).then_inc(dst_done, 1)

            def low(e):
                low_gate_up(v, e)
                low_down(v, e).then_inc(w_lo_dve, 1)

            v.memset(b_rows[:].bitcast(I32), 0).then_inc(brow_zero, 1)
            v.memset(blk[:].rearrange("p g m b d -> p (g m b d)"), 0.0).then_inc(blk_zero, 1)
            v.memset(chosen[:, B, :], 0.0)
            v.memset(expert_i[:, T:T + 1], 0)
            for g in range(GN):
                v.wait_ge(x_in[g], 16)
                stats_of(xs, g)
            variance((0, 1), 0)

            def factor(dst_, a, c, f):
                for m in range(2):
                    ins = v.tensor_scalar(dst_[:, m, :], row[:, a, m, :], col[:, c + m:c + m + 1], f, ALU.mult, ALU.mult)
                ins.then_inc(factors, 1)

            v.wait_ge(small_in, 16)
            factor(bqk, 0, 2, 1.0)
            factor(bqb, 1, 2, float(P))
            for g in range(GN):
                normed(xs, xn, g, g, xn_dve)
            factor(wqk, 0, 0, 1.0)
            factor(wqb, 1, 0, 1.0)
            step(v.tensor_copy(b_part[:, 0], b_raw[:]))
            step(v.tensor_tensor(b_rest[:, 0], b_raw[:], b_part[:, 0], ALU.subtract))
            step(v.tensor_copy(b_part[:, 1], b_rest[:, 0]))
            step(v.tensor_tensor(b_rest[:, 1], b_rest[:, 0], b_part[:, 1], ALU.subtract))
            v.tensor_copy(b_part[:, 2], b_rest[:, 1]).then_inc(b_split, 1)

            def by_head(a):
                return a.unsqueeze(2).to_broadcast([D, 2, GB, HD])

            def flat(a, g):
                return a[:, g].rearrange("p m b j -> p (m b) j")

            def over(a, g):
                return a[:, g].unsqueeze(2).to_broadcast([D, 2 * GB, HD])

            for g in range(GN):
                v.wait_ge(g_ps, GB * (g + 1))
                v.tensor_copy(part(xsum, g).rearrange("p (k b) -> p k b", k=2), G[g][:, :, :, D]).then_inc(xsum_sb, 1)
                for h in (0, 1):
                    hs = slice(h * HD, (h + 1) * HD)
                    last[g] = mark(v.tensor_copy(gsel[hs, g * GB:(g + 1) * GB].rearrange("p (k b) j -> p k b j", k=2),
                                                 G[g][hs, :, :, hs]))
            def scores(g):
                v.wait_ge(g_act, 2 * (g + 1))
                return v.tensor_tensor(s[:, g], part(gsel, g).unsqueeze(1).to_broadcast([D, 2, GB, HD]), by_head(wqk[:]), ALU.mult)

            v.wait_ge(factors, 4)
            both(scores)

            def ctx_part(g):
                v.wait_ge(uq_done, g + 1)
                return v.tensor_tensor(s[:, g], s[:, g], uq[:, g], ALU.add)

            both(ctx_part)

            def sum_part(g):
                v.wait_ge(t2_done, g + 1)
                return v.tensor_tensor(s[:, g], s[:, g], t2[:, g], ALU.add)

            both(sum_part)
            both(lambda g: v.tensor_reduce(smax[:, g], flat(s, g), AX, ALU.max))
            for g in range(GN):
                after(last[g])
                v.tensor_tensor(flat(s, g), flat(s, g), over(smax, g), ALU.subtract).then_inc(s_done, 1)

            low(DVE_LOWS[0])

            def total(g):
                v.wait_ge(exp_done, g + 1)
                return v.tensor_reduce(rsum[:, g], flat(s, g), AX, ALU.add)

            both(total)
            both(lambda g: v.reciprocal(rsum[:, g], rsum[:, g]))
            both(lambda g: v.tensor_scalar(rsum[:, g], rsum[:, g], col[:, 4:5], 2.0, ALU.mult, ALU.mult))
            for g in range(GN):
                after(last[g])
                v.tensor_tensor(flat(s, g), flat(s, g), over(rsum, g), ALU.mult).then_inc(attn_done, 1)
            for g in range(GN):
                v.wait_ge(attn_done, g + 1)
                last[g] = mark(v.tensor_tensor(mv[:, g], s[:, g], by_head(row[:, 2]), ALU.mult))
            both(lambda g: v.tensor_tensor(mr[:, g, 0], mv[:, g, 0], mv[:, g, 1], ALU.add))
            for g in range(GN):
                v.wait_ge(r_done, g + 1)
                after(last[g])
                v.transpose(mrT[:, g].rearrange("p m b j -> p (m b j)"),
                            mr[:, g].rearrange("p m b j -> p (m b j)")).then_inc(mrT_done, 1)
            v.wait_ge(blk_zero, 1)
            for g in range(GN):
                v.wait_ge(mrT_done, g + 1)
                for h in (0, 1):
                    hs = slice(h * HD, (h + 1) * HD)
                    v.tensor_copy(blk[hs, g, :, :, hs].rearrange("p m b d -> p (m b) d"),
                                  mrT[hs, g].rearrange("p m b d -> p (m b) d")).then_inc(blk_dve, 1)
            v.wait_ge(ones_col, 4)
            step(v.tensor_scalar(row_no[:], row_no[:], E - 1, None, ALU.bitwise_and))
            v.wait_ge(consts, 7)
            v.tensor_scalar(pick[:], tile_no[:, 0:E].unsqueeze(2).to_broadcast([P, E, P]), row_no[:, 0:1], None,
                            ALU.is_equal).then_inc(pick_done, 1)
            for g in range(GN):
                v.wait_ge(att_ps, g + 1)
                v.tensor_tensor(part(x1, g), part(xs, g), ATT[g], ALU.add).then_inc(x1_done, 1)
                v.wait_ge(x1_done, g + 1)
                stats_of(x1, g)
                variance((g,), GN)
            for g in range(GN):
                normed(x1, xn2, g, GN + g, xn2_dve)

            low(DVE_LOWS[1])
            low(DVE_LOWS[2])
            v.wait_ge(consts, N_CONST)
            for g in range(GN):
                v.wait_ge(logit_ps, g + 1)
                last[g] = mark(v.tensor_reduce(part(lmax, g), LOGIT[g], AX, ALU.max))
            for g in range(GN):
                after(last[g])
                v.tensor_tensor(part(logit, g), LOGIT[g], part(lmax, g).unsqueeze(2).to_broadcast([P, GB, E]),
                                ALU.subtract).then_inc(logit_sb, 1)
            ranks = rank_no[:].unsqueeze(1).to_broadcast([P, GB, E])

            def wide(a, g):
                return part(a, g).unsqueeze(2).to_broadcast([P, GB, E])

            for g in range(GN):
                v.wait_ge(logit_sb, g + 1)
                last[g] = mark(v.scalar_tensor_tensor(out=part(key, g), in0=part(logit, g), scalar=0.0, in1=ranks,
                                                      op0=ALU.is_equal, op1=ALU.mult))
            both(lambda g: v.tensor_reduce(part(kmax, g), part(key, g), AX, ALU.max))
            both(lambda g: v.tensor_tensor(part(mask[:, 0], g), part(key, g), wide(kmax, g), ALU.is_equal))
            both(lambda g: v.scalar_tensor_tensor(out=part(second, g), in0=part(mask[:, 0], g), scalar=-3.0e38,
                                                  in1=part(logit, g), op0=ALU.mult, op1=ALU.add))
            both(lambda g: v.tensor_reduce(part(lmax, g), part(second, g), AX, ALU.max))
            both(lambda g: v.tensor_tensor(part(key, g), part(second, g), wide(lmax, g), ALU.is_equal))
            both(lambda g: v.tensor_tensor(part(key, g), part(key, g), ranks, ALU.mult))
            both(lambda g: v.tensor_reduce(part(kmax, g), part(key, g), AX, ALU.max))
            both(lambda g: v.tensor_tensor(part(mask[:, 1], g), part(key, g), wide(kmax, g), ALU.is_equal))
            for g in range(GN):
                after(last[g])
                v.tensor_tensor(part(chosen, g), part(mask[:, 0], g), part(mask[:, 1], g), ALU.add).then_inc(chosen_done, 1)
            for g in range(GN):
                v.wait_ge(pexp_done, g + 1)
                last[g] = mark(v.tensor_reduce(part(psum_e, g), part(prob, g), AX, ALU.add))

            v.wait_ge(place_ps, 1)
            step(v.tensor_tensor(cmp[:], PLACE[:, B, :].unsqueeze(2).to_broadcast([P, E, B]),
                                 tile_edge[:, 0:B].unsqueeze(1).to_broadcast([P, E, B]), ALU.is_gt))
            step(v.tensor_reduce(ntile[:], cmp[:], AX, ALU.add))
            step(v.tensor_tensor(cmp[:], lower_p[:], ntile[:].unsqueeze(1).to_broadcast([P, E, E]), ALU.mult))
            step(v.tensor_reduce(first[:], cmp[:], AX, ALU.add))
            step(v.tensor_tensor(place[:], PLACE[:, 0:B, :], first[:].unsqueeze(1).to_broadcast([P, B, E]), ALU.add))
            step(v.tensor_tensor(prod[:], mask[:], place[:].unsqueeze(1).to_broadcast([P, K, B, E]), ALU.mult))
            with nc.allow_low_precision(reason="whole numbers under 2^24"):
                step(v.tensor_reduce(slot_i[:].rearrange("p (k b) -> p k b", k=K), prod[:], AX, ALU.add))
            v.tensor_scalar(lane_i[:], slot_i[:], P - 1, None, ALU.bitwise_and).then_inc(lane_done, 1)
            step(v.tensor_scalar(tile_i[:], slot_i[:], 7, None, ALU.logical_shift_right))
            v.tensor_tensor(in_tile[:], tile_i[:].unsqueeze(2).to_broadcast([P, K * B, T]),
                            tile_no[:].unsqueeze(1).to_broadcast([P, K * B, T]), ALU.is_equal).then_inc(in_tile_done, 1)
            v.wait_ge(in_tile_done, 1)
            v.tensor_tensor(tile_rhs[:, :, 0, :], in_tile[:],
                            src_id[:].rearrange("p k b -> p (k b)").unsqueeze(2).to_broadcast([P, K * B, T]),
                            ALU.mult).then_inc(tile_rhs_done, 1)
            v.wait_ge(lane_done, 1)
            for m in range(K * B - LANES_POOL):
                v.tensor_scalar(lane_lhs[:, m, :], lane_no[:], lane_i[:, m:m + 1], None, ALU.is_equal).then_inc(lane_dve, 1)
            step(v.scalar_tensor_tensor(out=past[:], in0=ntile[:], scalar=float(P), in1=first[:], op0=ALU.mult, op1=ALU.add))
            step(v.tensor_tensor(cmp_t[:], tile_edge[:].unsqueeze(2).to_broadcast([P, T, E]),
                                 past[:].unsqueeze(1).to_broadcast([P, T, E]), ALU.is_ge))
            step(v.tensor_reduce(expert[:], cmp_t[:], AX, ALU.add))
            v.tensor_scalar(expert_i[:, 0:T], expert[:], E - 1.0, None, ALU.min).then_inc(experts_done, 1)
            v.wait_ge(inv_ps, 1)
            v.tensor_copy(src_i[:], INV[:, 0, :]).then_inc(src_done, 1)
            step(v.tensor_copy(dst[:], INV[:, 1, :]))
            mark(v.scalar_tensor_tensor(out=pad[:], in0=dst[:], scalar=0.0, in1=pad_row[:], op0=ALU.is_equal, op1=ALU.mult))
            step(v.scalar_tensor_tensor(out=dst[:], in0=INV[:, 0, :], scalar=2.0, in1=dst[:], op0=ALU.mult, op1=ALU.add))
            step(v.tensor_tensor(dst[:], dst[:], pad[:], ALU.add))
            v.tensor_scalar(dst_i[:], dst[:], 1.0, None, ALU.subtract).then_inc(dst_done, 1)
            low(DVE_LOWS[3])
            step(v.reciprocal(psum_e[:], psum_e[:]))
            step(v.tensor_tensor(prob[:], prob[:], psum_e[:].unsqueeze(2).to_broadcast([P, B, E]), ALU.mult))
            step(v.tensor_tensor(gated[:], mask[:], prob[:].unsqueeze(1).to_broadcast([P, K, B, E]), ALU.mult))
            gates = mark(v.tensor_reduce(gate[:], gated[:], AX, ALU.add))

            def turn(s, i, q):
                if real(s):
                    v.wait_ge(up_ps, s + 1)
                    v.wait_ge(act_done, s + 1)
                    if again(s):
                        v.wait_ge(hT_ps, s - 1)
                    v.tensor_tensor(hid[:, q, :], pU[q], act[:, q, :], ALU.mult).then_inc(hid_done, 1)
                if real(s - 1):
                    v.wait_ge(hT_hi_done, s)
                    if again(s - 1):
                        v.wait_ge(y_ps, s - 2)
                    v.tensor_tensor(hT_lo[:, 1 - q], pH[1 - q], hT_hi[:, 1 - q].bitcast(F32),
                                    ALU.subtract).then_inc(hT_lo_done, 1)
                if real(s + 2):
                    v.wait_ge(xT_hi_done, s + 3)
                    if again(s + 2):
                        v.wait_ge(up_ps, s + 1)
                    v.tensor_tensor(xT_lo[:, q, :], pX, xT_hi[:, q, :].bitcast(F32), ALU.subtract).then_inc(xT_lo_done, 1)
                if real(s - 2):
                    v.wait_ge(y_ps, s - 1)
                    if again(s - 2):
                        v.wait_ge(scattered[q], (s - 2 - q) * 8)
                    v.tensor_reduce(y[:, q, :], pY.rearrange("p (c d) -> p d c", c=2), AX, ALU.add).then_inc(y_done, 1)

            pipeline(v, turn)

            after(gates)
            for i in range(4):
                v.wait_ge(res_in[i], 16)
                for b in (2 * i, 2 * i + 1):
                    k = mark(v.scalar_tensor_tensor(out=fin[:, b, :], in0=res[:, b, 0, :], scalar=gate[:, 0, b:b + 1],
                                                    in1=x1[:, b, :], op0=ALU.mult, op1=ALU.add))
                after(k)
                for b in (2 * i, 2 * i + 1):
                    ins = v.scalar_tensor_tensor(out=fin[:, b, :], in0=res[:, b, 1, :], scalar=gate[:, 1, b:b + 1],
                                                 in1=fin[:, b, :], op0=ALU.mult, op1=ALU.add)
                ins.then_inc(fin_done, 1)

        @block.tensor
        def _(pe):
            def warm(n, bank):
                for _ in range(n):
                    pe.matmul(ps[:, bank, :], ones_bf[:], ones_bf[:].unsqueeze(1).to_broadcast([P, 4, P]), start=True, stop=True)

            pe.wait_ge(ones_col, 4)
            warm(8, 6)
            pe.wait_ge(ones_col, 4)
            pe.wait_ge(c_in, 16)
            for i in range(2):
                pe.matmul(ps[:, 4 + i, :], ones[:], cn[:, 4 * i:4 * i + 4, 0:D],
                          start=True, stop=True).then_inc(csum_ps, 1)
            for b in range(B):
                pe.wait_ge((xn_dve, xn_act)[b % 2], b // 2 + 1)
                pe.matmul(G[b // GB][:, b % GB // 2, b % 2, :], xn[:, b, :], cn[:, b, :], start=True, stop=True).then_inc(g_ps, 1)
            pe.wait_ge(bp_in, 16)
            for g in range(GN):
                pe.matmul(ATT[g], ones[0:1, :], bp[:].unsqueeze(1).to_broadcast([1, GB, D]), start=True, stop=False)
            pe.wait_ge(cT_in, 16)
            pe.wait_ge(csum_sb, 4)
            pe.wait_ge(s_done, 1)
            warm(16, 4)
            for g in range(GN):
                pe.wait_ge(blk_dve, 2 * (g + 1))
                pe.wait_ge(blk_act, 2 * (g + 1))
                pe.matmul(ps[:, 6 + g, :], ones[:], blk[:, g, 1].rearrange("p b d -> p (b d)"), start=False, stop=False)
                for b in range(GB):
                    mm = pe.matmul(ATT[g][:, b, :], cT[:, g * GB + b, :], blk[:, g, 0, b, :], start=False, stop=(b == GB - 1))
                mm.then_inc(att_ps, 1)
            warm(8, 4)
            pe.wait_ge(consts, N_CONST)
            for g in range(GN):
                for b in range(g * GB, (g + 1) * GB):
                    pe.wait_ge((xn2_dve, xn2_act)[b % 2], b // 2 + 1)
                    pe.transpose(XN2T[g][:, b % GB, :], xn2[:, b, :], ident[:]).then_inc(xn2T_ps, 1)
            for g in range(GN):
                pe.wait_ge(xn2T_sb, g + 1)
                for b in range(GB):
                    mm = pe.matmul(LOGIT[g][:, b, :], xn2T[:, g * GB + b, :], rw[:], start=True, stop=True)
                mm.then_inc(logit_ps, 1)
            pe.wait_ge(chosen_done, GN)
            pe.matmul(PLACE, before[:], chosen[:], start=True, stop=False)
            for b in range(B):
                mm = pe.matmul(PLACE[:, b + 1:B + 1, :], ones_bf[:],
                               chosen[:, b, :].unsqueeze(1).to_broadcast([P, B - b, E]), start=False, stop=(b == B - 1))
            mm.then_inc(place_ps, 1)
            pe.wait_ge(x1_done, GN)
            warm(10, 7)
            pe.wait_ge(tile_rhs_done, 1)
            pe.wait_ge(tile_rhs_act, K)
            order = list(range(K * B - LANES_POOL)) + list(range(K * B - LANES_POOL, K * B))
            for m in order:
                if m < K * B - LANES_POOL:
                    pe.wait_ge(lane_dve, m + 1)
                else:
                    pe.wait_ge(lane_pool, m + 1 - (K * B - LANES_POOL))
                mm = pe.matmul(INV, lane_lhs[:, m, :], tile_rhs[:, m], start=(m == order[0]), stop=(m == order[-1]))
            mm.then_inc(inv_ps, 1)
            warm(12, 7)

            pe.wait_ge(experts_done, 1)
            pe.wait_ge(brow_in, 16)
            pe.wait_ge(pick_done, 1)
            pe.wait_ge(w_lo_pool, E - len(DVE_LOWS))
            pe.wait_ge(w_lo_dve, len(DVE_LOWS))

            def expert_of(t):
                return nc.values_load(expert_i[0:1, bass.ds(t, 1)], engines=(mybir.EngineType.PE,), min_val=0, max_val=E - 1,
                                      skip_runtime_bounds_check_because="a count of at most E, cut to E - 1")

            def turn(s, i, q):
                e_down = expert_of(s - 2) if real(s - 2) else None
                if real(s - 1):
                    pe.wait_ge(hid_done, s)
                    if again(s - 1):
                        pe.wait_ge(hT_lo_done, s - 2)
                    for c in range(FC):
                        mm = pe.transpose(pH[1 - q][:, c, :], hid[:, 1 - q, c * P:(c + 1) * P], ident[:])
                    mm.then_inc(hT_ps, 1)
                if real(s - 2):
                    e = e_down
                    pe.wait_ge(hT_lo_done, s - 1)
                    if again(s - 1):
                        pe.wait_ge(y_done, s - 2)
                    for c in range(FC):
                        pe.matmul(pY, hT_hi[:, q, c, :], w_down[:, e, c].rearrange("p h d -> p (h d)"),
                                  start=(c == 0), stop=False)
                    for c in range(FC):
                        pe.matmul(pY[:, 0:D], hT_lo[:, q, c, :], w_down[:, e, c, 0, :], start=False, stop=False)
                    pe.matmul(pY[:, 0:D], pick[:, e, :], b_rows[:, 2 * F:BW], start=False, stop=True).then_inc(y_ps, 1)
                if real(s + 2):
                    x = (i + 2) % XG
                    pe.wait_ge(gathered[x], (s + 2 - x) * (16 // XG) + 16)
                    if again(s + 3):
                        pe.wait_ge(xT_lo_done, s + 2)
                    pe.transpose(pX, xg[:, x, :], ident[:]).then_inc(xT_ps, 1)
                if real(s + 1):
                    e = expert_of(s + 1)
                    pe.wait_ge(xT_lo_done, s + 2)
                    for c0, psum, used, ready in ((0, pG[1 - q], act_done, gate_ps), (F, pU[1 - q], hid_done, up_ps)):
                        if again(s + 1):
                            pe.wait_ge(used, s)
                        pe.matmul(psum, pick[:, e, :], b_rows[:, c0:c0 + F], start=True, stop=False)
                        pe.matmul(psum, xT_hi[:, 1 - q, :], w_lo[:, e, c0:c0 + F], start=False, stop=False)
                        pe.matmul(psum, xT_hi[:, 1 - q, :], w_hi[:, e, c0:c0 + F], start=False, stop=False)
                        pe.matmul(psum, xT_lo[:, 1 - q, :], w_hi[:, e, c0:c0 + F], start=False, stop=True).then_inc(ready, 1)

            pipeline(pe, turn)


def kernel(**inputs):
    import numpy as np
    import concourse.bacc as bacc
    from concourse.bass_utils import run_bass_kernel_spmd as run

    a = {k.replace("L0_xattn_", "").replace("L0_ffn_", ""): np.asarray(v) for k, v in inputs.items()}
    cols = np.stack([a[k] for k in ("wqg", "wql", "bqg", "bql", "wp")], axis=1)
    rows = np.stack([a[k].reshape(H, HD) for k in ("wkg", "wkl", "bkg", "bkl", "wvg", "wvl", "bvg", "bvl")], axis=1)
    rows = np.repeat(rows.reshape(H, 8 * HD), HD, axis=0)
    wpack = np.concatenate([
        a["wg_w"].transpose(2, 0, 1), a["w1_w"].transpose(2, 0, 1),
        a["w2_w"].reshape(E, D, FC, P).transpose(3, 0, 2, 1).reshape(P, E, FC * D)], axis=2)
    bias = np.concatenate([a["wg_b"], a["w1_b"], a["w2_b"]], axis=1)
    arrays = {
        "x": a["x"], "ctxn": a["ctx_1024"], "ctxT": a["ctx_1024"].transpose(2, 0, 1),
        "small_pack": np.concatenate([rows, cols, a["router_w"].T, bias.reshape(P, E * BW // P)], axis=1),
        "bp_row": a["bp"].reshape(1, D), "wpack": wpack,
    }
    arrays = {k: np.ascontiguousarray(v) for k, v in arrays.items()}
    nc = bacc.Bacc("TRN2", target_bir_lowering=False, num_devices=1)
    args = [nc.dram_tensor(k, v.shape, F32, kind="ExternalInput").ap() for k, v in arrays.items()]
    out = nc.dram_tensor("out", (B, P, D), F32, kind="ExternalOutput").ap()
    program(nc, *args, out)
    r = run(nc, [arrays], core_ids=[0])
    return r.results[0]["out"]
```

```python
from contextlib import ExitStack

import concourse.bass as bass
from concourse import mybir

F32 = mybir.dt.float32
F32R = mybir.dt.float32r
BF16 = mybir.dt.bfloat16
F16 = mybir.dt.float16
I32 = mybir.dt.int32
ALU = mybir.AluOpType
ACT = mybir.ActivationFunctionType
AX = mybir.AxisListType.X

P = 128
B = 8
D = 128
H = 4
HD = D // H
E = 8
F = 512
FC = F // P
K = 2
W3 = 2 * F + FC * D
BW = F + D
SMALL = 8 * HD + 5 + E + E * BW // P
PAIRS = K * B * P
T = (PAIRS + E * (P - 1)) // P
SCALE = float(D) ** -0.5
EPS = 1e-5
XG = 4
LG = 4
GN = 2
GB = B // GN
PARTS = 3


def program(nc, x, ctxn, ctxT, small_pack, bp_row, up_bias, wpack, out):
    with ExitStack() as st:
        def sb(name, shape, dt=F32):
            return st.enter_context(nc.sbuf_tensor(name, shape, dt))

        def sem(name):
            return st.enter_context(nc.semaphore(name))

        def dram(name, shape, dt=F32):
            return nc.dram_tensor(name, shape, dt, kind="Internal").ap()

        tokens_dram = dram("tokens_dram", [P * B, D])
        results_dram = dram("results_dram", [PAIRS + T * P, D])
        parts_dram = dram("parts_dram", [PARTS, E * BW], BF16)

        ident = sb("ident", [P, P])
        ones = sb("ones", [P, P])
        ones_bf = sb("ones_bf", [P, P], BF16)
        before = sb("before", [P, P], BF16)
        lower = sb("lower", [P, E, E])
        tile_edge = sb("tile_edge", [P, B])
        tile_no = sb("tile_no", [P, T])
        tile_rep = sb("tile_rep", [P, T, K * B], F16)
        lane_rep = sb("lane_rep", [P, P, LG], F16)
        src_id = sb("src_id", [P, K, B], F16)
        pad_row = sb("pad_row", [P, T])
        rank_no = sb("rank_no", [P, E])
        row_no = sb("row_no", [P, 1], I32)
        pick = sb("pick", [P, E, P], BF16)
        minus_half = sb("minus_half", [P, B])

        xs = sb("xs", [P, B, D])
        CW = D + 1
        cc = sb("cc", [P, B * (CW + P)])
        cn = cc[:, 0:B * CW].rearrange("p (b d) -> p b d", d=CW)
        cT = cc[:, B * CW:].rearrange("p (b n) -> p b n", n=P)
        small = sb("small", [P, SMALL])
        row = small[:, 0:8 * HD].rearrange("p (a g j) -> p a g j", a=4, g=2)
        col = small[:, 8 * HD:8 * HD + 5]
        rw = small[:, 8 * HD + 5:8 * HD + 5 + E]
        b_raw = small[:, 8 * HD + 5 + E:SMALL]
        bp = sb("bp", [1, D])
        xn = sb("xn", [P, B, D])
        xc = xn
        x1 = sb("x1", [P, B, D])
        stats = sb("stats", [P, B, 6])
        mean = sb("mean", [P, B])
        half = sb("half", [P, B])
        var = sb("var", [P, B])
        rstd = sb("rstd", [P, B])
        wqk = sb("wqk", [D, 2, HD])
        bqk = sb("bqk", [D, 2, HD])
        bq_sum = sb("bq_sum", [D, 2])
        qsum = sb("qsum", [D, 2, B])
        csum = sb("csum", [D, B, HD])
        gsel = sb("gsel", [D, B, HD])
        xsum = sb("xsum", [D, B])
        nmr = sb("nmr", [P, B])
        uq = sb("uq", [D, GN, 2, GB, HD])
        t2 = sb("t2", [D, GN, 2, GB, HD])
        s = sb("s", [D, GN, 2, GB, HD])
        smax = sb("smax", [D, GN, 2 * GB])
        rsum = sb("rsum", [D, GN, 2 * GB])
        mv = sb("mv", [D, GN, 2, GB, HD])
        mr = sb("mr", [D, GN, 2, GB, HD])
        mrT = sb("mrT", [D, GN, 2, GB, HD])
        blk = sb("blk", [D, GN, 2, GB, D])
        xn2 = sb("xn2", [P, B, D])
        xcT = xs

        prob = sb("prob", [P, B, E])
        lmax = sb("lmax", [P, B])
        logit = sb("logit", [P, B, E])
        second = sb("second", [P, B, E])
        key = sb("key", [P, B, E])
        kmax = sb("kmax", [P, B])
        psum_e = sb("psum_e", [P, B])
        chosen = sb("chosen", [P, B + 1, E], BF16)
        mask = sb("mask", [P, K, B, E])
        prod = sb("prod", [P, K, B, E])
        gated = sb("gated", [P, K, B, E])
        gate = sb("gate", [P, K, B])
        ahead_i = sb("ahead_i", [P, K * B], I32)
        digit_i = sb("digit_i", [P, 2, K * B], I32)
        digit = sb("digit", [P, 2, K * B], F16)
        start = sb("start", [P, K * B], F16)
        cmp = sb("cmp", [P, E, B])
        ntile = sb("ntile", [P, E])
        first = sb("first", [P, E])
        past = sb("past", [P, E])
        cmp_t = sb("cmp_t", [P, T, E])
        expert = sb("expert", [P, T])
        expert_i = sb("expert_i", [P, T + 1], I32)
        in_tile = sb("in_tile", [P, T, K * B], F16)
        tile_rhs = sb("tile_rhs", [P, 2, T, K * B], F16)
        lane_lhs = sb("lane_lhs", [P, K * B // LG, P, LG], F16)
        dst = sb("dst", [P, T])
        pad = sb("pad", [P, T])
        src_i = sb("src_i", [P, T], I32)
        dst_i = sb("dst_i", [P, T], I32)

        w_hi = sb("w_hi", [P, E, 2 * F], F32R)
        w_lo = sb("w_lo", [P, E, 2 * F], F32R)
        w_down = sb("w_down", [P, E, FC, 2, D], F32R)
        b_up = sb("b_up", [P, E, F])
        b_part = sb("b_part", [P, PARTS, E * BW // P], BF16)
        b_rest = sb("b_rest", [P, PARTS - 1, E * BW // P])
        b_rows = sb("b_rows", [P, BW], BF16)
        xg = sb("xg", [P, XG, D])
        xT_hi = sb("xT_hi", [D, 2, P], F32R)
        xT_lo = sb("xT_lo", [D, 2, P], F32R)
        act = sb("act", [P, 2, F])
        hid = sb("hid", [P, 2, F])
        hT_hi = sb("hT_hi", [P, 2, FC, P], F32R)
        hT_lo = sb("hT_lo", [P, 2, FC, P], F32R)
        y = sb("y", [P, 3, D])
        res = cc[:, 0:B * K * D].rearrange("p (b k d) -> p b k d", b=B, k=K)
        fin = xn

        ps = st.enter_context(nc.psum_tensor("ps", [P, 8, 512], F32))
        G = [ps[:, 2 * g:2 * g + 2, 0:2 * CW].rearrange("p k (b d) -> p k b d", d=CW) for g in range(GN)]
        CSUM = ps[:, 4:6, :].rearrange("p k (b d) -> p (k b) d", d=D)
        ATT = [ps[:, 4:6, 0:2 * D].rearrange("p k (b d) -> p k b d", d=D),
               ps[:, 7, :].rearrange("p (k b d) -> p k b d", k=2, d=D)]
        ATT_BANKS = ((4, 0, 2), (5, 2, 2), (7, 4, 4))
        XCT = [ps[:, i, 0:2 * D].rearrange("p (b d) -> p b d", d=D) for i in range(B // 2)]
        LOGIT = [ps[:, 6, g * GB * E:(g + 1) * GB * E].rearrange("p (b e) -> p b e", e=E) for g in range(GN)]
        PLACE = ps[:, 4, 0:(B + 1) * E].rearrange("p (b e) -> p b e", e=E)
        INV = ps[:, 5, 0:2 * T].rearrange("p (c t) -> p c t", t=T)
        pG = [ps[:, 0, :], ps[:, 1, :]]
        pU = [ps[:, 2, :], ps[:, 3, :]]
        pH = [ps[:, 4, :].rearrange("p (c n) -> p c n", n=P), ps[:, 5, :].rearrange("p (c n) -> p c n", n=P)]
        pX = ps[:, 6, 0:P]
        pY = ps[:, 7, 0:2 * D]
        pY_free = ps[:, 6, 0:2 * D]

        x_in = [sem("x_in0"), sem("x_in1")]
        c_in = sem("c_in"); cT_in = sem("cT_in"); small_in = sem("small_in")
        b_out = sem("b_out"); brow_in = sem("brow_in"); brow_zero = sem("brow_zero")
        bp_in = sem("bp_in"); b_up_in = sem("b_up_in"); up_done = sem("up_done")
        w_in = [sem(f"w_in{e}") for e in range(E)]
        w_hi_done = sem("w_hi_done"); w_lo_pool = sem("w_lo_pool"); w_lo_dve = sem("w_lo_dve")
        b_split = sem("b_split")
        pool_step = sem("pool_step"); dve_step = sem("dve_step")
        consts = sem("consts"); ones_bf_done = sem("ones_bf_done"); ident_done = sem("ident_done")
        ones_col = sem("ones_col"); blk_zero = sem("blk_zero"); pick_done = sem("pick_done")
        mean_done = sem("mean_done"); xc_done = sem("xc_done"); scaled = sem("scaled")
        factors = sem("factors"); csum_ps = sem("csum_ps"); csum_sb = sem("csum_sb")
        uq_done = sem("uq_done")
        var_done = sem("var_done"); rstd_done = sem("rstd_done"); nmr_done = sem("nmr_done")
        xn_dve = sem("xn_dve"); xn_act = sem("xn_act")
        g_ps = sem("g_ps"); g_act = sem("g_act"); xsum_sb = sem("xsum_sb"); t2_done = sem("t2_done")
        s_done = sem("s_done"); exp_done = sem("exp_done"); attn_done = sem("attn_done")
        r_done = sem("r_done"); mrT_done = sem("mrT_done"); blk_act = sem("blk_act"); blk_dve = sem("blk_dve")
        att_ps = sem("att_ps"); xn2_done = sem("xn2_done"); tokens_out = sem("tokens_out")
        x1_done = sem("x1_done")
        xcT_ps = sem("xcT_ps"); xcT_sb = sem("xcT_sb"); logit_ps = sem("logit_ps")
        logit_sb = sem("logit_sb"); pexp_done = sem("pexp_done")
        chosen_done = sem("chosen_done"); place_ps = sem("place_ps"); experts_done = sem("experts_done")
        lane_done = sem("lane_done"); in_tile_done = sem("in_tile_done")
        tile_rhs_act = sem("tile_rhs_act"); tile_rhs_done = sem("tile_rhs_done")
        inv_ps = sem("inv_ps"); src_done = sem("src_done"); dst_done = sem("dst_done")
        gathered = [sem(f"gathered{i}") for i in range(XG)]
        scattered = [sem("scattered0"), sem("scattered1")]
        xT_ps = sem("xT_ps"); xT_hi_done = sem("xT_hi_done"); xT_lo_done = sem("xT_lo_done")
        gate_ps = sem("gate_ps"); up_ps = sem("up_ps"); act_done = sem("act_done"); hid_done = sem("hid_done")
        hT_ps = sem("hT_ps"); hT_hi_done = sem("hT_hi_done"); hT_lo_done = sem("hT_lo_done")
        y_ps = sem("y_ps"); y_done = sem("y_done")
        res_in = [sem(f"res_in{i}") for i in range(4)]
        gate_done = sem("gate_done"); second_gated = sem("second_gated")
        first_added = sem("first_added"); fin_done = [sem(f"fin_done{i}") for i in range(4)]
        out_done = sem("out_done")

        N_CONST = 9

        def chunks(a):
            return a.rearrange("p (c d) -> p c d", d=D)

        def low_gate_up(eng, e, cs=slice(0, 2 * F)):
            eng.wait_ge(w_hi_done, e + 1)
            return eng.tensor_tensor(w_lo[:, e, cs], w_lo[:, e, cs].bitcast(F32), w_hi[:, e, cs].bitcast(F32),
                                     ALU.subtract)

        def pairs_of(a, g):
            return a[:, g * GB:(g + 1) * GB, :].rearrange("p (k b) d -> p k b d", k=2)

        def low_down(eng, e, cs=slice(0, FC)):
            eng.wait_ge(w_hi_done, e + 1)
            return eng.tensor_tensor(w_down[:, e, cs, 1, :], w_down[:, e, cs, 1, :].bitcast(F32),
                                     w_down[:, e, cs, 0, :].bitcast(F32), ALU.subtract)

        def add_second(eng, i):
            eng.wait_ge(first_added, i + 1)
            eng.wait_ge(second_gated, i + 1)
            bs = slice(2 * i, 2 * i + 2)
            return eng.tensor_tensor(fin[:, bs], fin[:, bs], res[:, bs, 1, :], ALU.add).then_inc(fin_done[i], 1)

        UNROLL = XG
        HEAD = 4
        TAIL = HEAD + (T - 1 - HEAD) // UNROLL * UNROLL

        def real(t):
            return not isinstance(t, int) or 0 <= t < T

        def again(t):
            return not isinstance(t, int) or t >= 2

        def pipeline(eng, turn):
            for s in range(-2, HEAD):
                turn(s, s % UNROLL, s % 2)
            with eng.Fori(HEAD, TAIL, UNROLL) as s:
                for i in range(UNROLL):
                    turn(s + i, i, i % 2)
            for s in range(TAIL, T + 2):
                turn(s, s % UNROLL, s % 2)

        def first_product(s):
            return isinstance(s, int) and s == -1

        def last_tile(t):
            return isinstance(t, int) and t == T - 1

        def last_but_one(t):
            return isinstance(t, int) and t == T - 2

        def expert_of(eng, t):
            return nc.values_load(expert_i[0:1, bass.ds(t, 1)], engines=(eng.engine,), min_val=0, max_val=E - 1,
                                  skip_runtime_bounds_check_because="a count of at most E, cut to E - 1")

        block = st.enter_context(nc.Block())

        @block.sync
        def _(sp):
            sp.dma_start(xs[:, 0:GB, :], x[0:GB].rearrange("b n d -> n b d")).then_inc(x_in[0], 16)
            sp.dma_start(cn[:, :, 0:D], ctxn.rearrange("b n d -> n b d")).then_inc(c_in, 16)
            for e in range(E):
                sp.dma_start(w_lo[:, e, :].bitcast(F32), wpack[:, e, 0:2 * F]).then_inc(w_in[e], 16)
                sp.dma_start(w_down[:, e, :, 1, :].bitcast(F32), chunks(wpack[:, e, 2 * F:W3])).then_inc(w_in[e], 16)
                if e == 2:
                    sp.dma_start(cT, ctxT).then_inc(cT_in, 16)
            sp.dma_start(b_up[:].rearrange("p e f -> p (e f)"),
                         up_bias.rearrange("e f -> (e f)").unsqueeze(0).to_broadcast([P, E * F])).then_inc(b_up_in, 16)
            sp.wait_ge(b_split, 1)
            sp.dma_start(parts_dram.rearrange("j (p c) -> p j c", p=P), b_part[:]).then_inc(b_out, 16)
            sp.wait_ge(b_out, 16)
            sp.wait_ge(brow_zero, 1)
            sp.dma_start(b_rows[0:PARTS * E, :], parts_dram.rearrange("j (e c) -> (j e) c", e=E)).then_inc(brow_in, 16)
            tokens = tokens_dram.rearrange("(n b) d -> n b d", b=B)
            for g in range(GN):
                sp.wait_ge(xn2_done, GB * (g + 1))
                gs = slice(g * GB, (g + 1) * GB)
                sp.dma_start(tokens[:, gs, :], xn2[:, gs, :]).then_inc(tokens_out, 16)
            sp.wait_ge(scattered[0], 16 * ((T + 1) // 2))
            sp.wait_ge(scattered[1], 16 * (T // 2))
            rows_of = results_dram[0:PAIRS, :].rearrange("(n b k) d -> n b k d", b=B, k=K)
            for i in range(0, 4, 2):
                sp.dma_start(res[:, 2 * i:2 * i + 2], rows_of[:, 2 * i:2 * i + 2]).then_inc(res_in[i], 16)
            for i in range(4):
                sp.wait_ge(fin_done[i], 1)
                sp.dma_start(out[2 * i:2 * i + 2].rearrange("b n d -> n b d"), fin[:, 2 * i:2 * i + 2, :]).then_inc(out_done, 16)
            sp.wait_ge(out_done, 64)

        @block.gpsimd
        def _(pool):
            done = [0]

            def step(ins):
                done[0] += 1
                ins.then_inc(pool_step, 1)
                pool.wait_ge(pool_step, done[0])

            def count(ap, pattern, base=0, per_row=0):
                pool.iota(ap, pattern, base=base, channel_multiplier=per_row,
                          allow_small_or_imprecise_dtypes=True).then_inc(consts, 1)

            pool.memset(ones_bf[:], 1.0).then_inc(ones_bf_done, 1)
            pool.memset(ones[:], 1.0).then_inc(ones_col, 1)
            pool.memset(cn[:, :, D:CW], 1.0).then_inc(ones_col, 1)
            pool.memset(minus_half[:], -0.5)
            pool.memset(before[:], 1.0)
            step(pool.memset(lower[:], 1.0))
            pool.affine_select(out=before[:], in_=before[:], compare_op=ALU.is_gt, fill=0.0, base=0,
                               pattern=[[1, P]], channel_multiplier=-1).then_inc(consts, 1)
            pool.affine_select(out=lower[:], in_=lower[:], compare_op=ALU.is_gt, fill=0.0, base=0,
                               pattern=[[1, E], [-1, E]], channel_multiplier=0).then_inc(consts, 1)
            pool.iota(row_no[:], [[0, 1]], base=0, channel_multiplier=1).then_inc(ones_col, 1)
            count(tile_edge[:], [[P, B]])
            count(tile_no[:], [[1, T]])
            count(tile_rep[:], [[1, T], [0, K * B]])
            count(lane_rep[:], [[1, P], [0, LG]])
            count(src_id[:], [[0, K], [1, B]], per_row=B)
            step(pool.memset(ident[:], 0.0))
            pool.affine_select(out=ident[:], in_=ident[:], compare_op=ALU.not_equal, fill=1.0, base=0,
                               pattern=[[-1, P]], channel_multiplier=1).then_inc(ident_done, 1)
            count(pad_row[:], [[P, T]], base=PAIRS + 1, per_row=1)
            count(rank_no[:], [[-1, E]], base=E)

            def low(e):
                low_gate_up(pool, e)
                low_down(pool, e).then_inc(w_lo_pool, 1)

            def inverse_root(n):
                g = n % GN
                pool.wait_ge(var_done, n + 1)
                gs = slice(g * GB, (g + 1) * GB)
                pool.tensor_tensor(rstd[:, gs], var[:, gs], minus_half[:, gs], ALU.pow).then_inc(rstd_done, 1)

            inverse_root(0)
            inverse_root(1)
            pool.wait_ge(factors, 1)
            pool.wait_ge(csum_sb, 4)
            for g in range(GN):
                cs = csum[:, g * GB:(g + 1) * GB].unsqueeze(1).to_broadcast([D, 2, GB, HD])
                pool.tensor_tensor(uq[:, g], cs, bqk[:].unsqueeze(2).to_broadcast([D, 2, GB, HD]),
                                   ALU.mult).then_inc(uq_done, 1)
            low(0)
            for g in range(GN):
                pool.wait_ge(attn_done, g + 1)
                pool.tensor_tensor(t2[:, g], s[:, g], row[:, 3].unsqueeze(2).to_broadcast([D, 2, GB, HD]),
                                   ALU.mult).then_inc(r_done, 1)
            low(1)
            low(2)
            low_down(pool, 3)
            inverse_root(2)
            inverse_root(3)
            low_gate_up(pool, 3).then_inc(w_lo_pool, 1)
            low(4)
            low_gate_up(pool, 7, slice(0, F)).then_inc(w_lo_pool, 1)

            def gather(t):
                if t >= XG:
                    pool.wait_ge(xT_ps, t + 1 - XG)
                pool.indirect_dma_start(xg[:, t % XG, :], None, tokens_dram,
                                        bass.IndirectOffsetOnAxis(ap=src_i[:, t:t + 1], axis=0)).then_inc(gathered[t % XG], 16)

            def scatter(t):
                pool.wait_ge(y_done, t + 1)
                pool.indirect_dma_start(results_dram, bass.IndirectOffsetOnAxis(ap=dst_i[:, t:t + 1], axis=0),
                                        y[:, 2 if last_tile(t) else t % 2, :], None).then_inc(scattered[t % 2], 16)

            pool.wait_ge(src_done, 1)
            pool.wait_ge(tokens_out, 32)
            for t in range(XG):
                gather(t)
            for t in range(T + 2):
                if t + XG < T:
                    gather(t + XG)
                if t == 2:
                    pool.wait_ge(dst_done, 1)
                if t >= 2:
                    scatter(t - 2)

            add_second(pool, 0)
            add_second(pool, 1)

        @block.scalar
        def _(sc):
            sc.dma_start(xs[:, GB:B, :], x[GB:B].rearrange("b n d -> n b d")).then_inc(x_in[1], 16)
            sc.dma_start(small[:], small_pack).then_inc(small_in, 16)
            sc.dma_start(bp[:], bp_row).then_inc(bp_in, 16)

            def high(e):
                sc.wait_ge(w_in[e], 32)
                sc.copy(w_hi[:, e, :], w_lo[:, e, :].bitcast(F32))
                sc.copy(w_down[:, e, :, 0, :], w_down[:, e, :, 1, :].bitcast(F32)).then_inc(w_hi_done, 1)

            for g in range(GN):
                sc.wait_ge(nmr_done, g + 1)
                for b in range(g * GB + 1, (g + 1) * GB, 2):
                    sc.activation(xn[:, b, :], xs[:, b, :], ACT.Identity, bias=nmr[:, b:b + 1],
                                  scale=rstd[:, b:b + 1]).then_inc(xn_act, 1)
            for g in range(GN):
                sc.wait_ge(xsum_sb, g + 1)
                for h in (2, 3):
                    hs = slice(h * HD, (h + 1) * HD)
                    sc.copy(gsel[hs, g * GB:(g + 1) * GB].rearrange("p (k b) j -> p k b j", k=2),
                            G[g][hs, :, :, hs]).then_inc(g_act, 1)
            sc.wait_ge(csum_ps, GN)
            for h in range(H):
                hs = slice(h * HD, (h + 1) * HD)
                sc.copy(csum[hs], CSUM[hs, :, hs]).then_inc(csum_sb, 1)
            high(0)
            high(1)
            for g in range(GN):
                sc.wait_ge(s_done, g + 1)
                sc.activation(s[:, g], s[:, g], ACT.Exp, scale=SCALE).then_inc(exp_done, 1)
            high(2)
            high(3)
            for g in range(GN):
                sc.wait_ge(mrT_done, g + 1)
                sc.wait_ge(blk_zero, 1)
                for h in (2, 3):
                    hs = slice(h * HD, (h + 1) * HD)
                    sc.copy(blk[hs, g, :, :, hs].rearrange("p m b d -> p (m b) d"),
                            mrT[hs, g].rearrange("p m b d -> p (m b) d")).then_inc(blk_act, 1)
            high(4)
            high(5)
            for g in range(GN):
                for i in (2 * g, 2 * g + 1):
                    sc.wait_ge(xcT_ps, i + 1)
                    sc.copy(xcT[:, 2 * i:2 * i + 2, :], XCT[i]).then_inc(xcT_sb, 1)
                sc.wait_ge(xc_done, g + 1)
                sc.copy(pairs_of(x1, g), ATT[g]).then_inc(x1_done, 1)
            high(6)
            for g in range(GN):
                sc.wait_ge(rstd_done, GN + g + 1)
                for b in range(g * GB, (g + 1) * GB):
                    sc.mul(xn2[:, b, :], xc[:, b, :], rstd[:, b:b + 1]).then_inc(xn2_done, 1)
            high(7)
            for g in range(GN):
                gs = slice(g * GB, (g + 1) * GB)
                sc.wait_ge(scaled, g + 1)
                sc.activation(prob[:, gs], prob[:, gs], ACT.Exp).then_inc(pexp_done, 1)
            sc.activation(act[:, 0, 0:1], minus_half[:, 0:1], ACT.Gelu)
            sc.wait_ge(in_tile_done, 1)
            for k in range(K):
                ks = slice(k * B, (k + 1) * B)
                sc.mul(tile_rhs[:, 1, :, ks], in_tile[:, :, ks], k + 1.0).then_inc(tile_rhs_act, 1)

            def turn(s, i, q):
                if real(s):
                    sc.wait_ge(gate_ps, s + 1)
                    if again(s):
                        sc.wait_ge(hid_done, s - 1)
                    sc.activation(act[:, q, :], pG[q], ACT.Gelu).then_inc(act_done, 1)
                if real(s - 1):
                    sc.wait_ge(hT_ps, s)
                    sc.copy(hT_hi[:, 1 - q], pH[1 - q]).then_inc(hT_hi_done, 1)
                if real(s + 2):
                    sc.wait_ge(xT_ps, s + 3)
                    sc.copy(xT_hi[:, q, :], pX).then_inc(xT_hi_done, 1)

            pipeline(sc, turn)

            sc.wait_ge(scattered[0], 16 * ((T + 1) // 2))
            sc.wait_ge(scattered[1], 16 * (T // 2))
            rows_of = results_dram[0:PAIRS, :].rearrange("(n b k) d -> n b k d", b=B, k=K)
            for i in range(1, 4, 2):
                sc.dma_start(res[:, 2 * i:2 * i + 2], rows_of[:, 2 * i:2 * i + 2]).then_inc(res_in[i], 16)
            sc.wait_ge(gate_done, 1)
            for i in range(4):
                sc.wait_ge(res_in[i], 16)
                sc.mul(res[:, 2 * i, 1, :], res[:, 2 * i, 1, :], gate[:, 1, 2 * i:2 * i + 1])
                sc.mul(res[:, 2 * i + 1, 1, :], res[:, 2 * i + 1, 1, :], gate[:, 1, 2 * i + 1:2 * i + 2]).then_inc(second_gated, 1)

        @block.vector
        def _(v):
            done = [0]

            def mark(ins):
                done[0] += 1
                ins.then_inc(dve_step, 1)
                return done[0]

            def after(n):
                v.wait_ge(dve_step, n)

            def step(ins):
                after(mark(ins))

            def both(op):
                for g in range(GN):
                    if last[g]:
                        after(last[g])
                    last[g] = mark(op(g))

            last = [0] * GN

            def part(a, g):
                return a[:, g * GB:(g + 1) * GB]


            def moments(g):
                st = part(stats, g)
                after(last[g])
                mark(v.tensor_tensor(part(half, g), st[:, :, 1], st[:, :, 4], ALU.subtract))
                k = mark(v.tensor_tensor(part(mean, g), st[:, :, 1], st[:, :, 4], ALU.add))
                last[g] = mark(v.tensor_tensor(part(var, g), st[:, :, 2], st[:, :, 5], ALU.add))
                after(k)
                v.tensor_scalar(part(mean, g), part(mean, g), 0.5, None, ALU.mult).then_inc(mean_done, 1)

            def variances():
                both(lambda g: v.scalar_tensor_tensor(out=part(half, g), in0=part(half, g), scalar=D / 4.0,
                                                      in1=part(half, g), op0=ALU.mult, op1=ALU.mult))
                both(lambda g: v.tensor_tensor(part(var, g), part(var, g), part(half, g), ALU.add))
                for g in range(GN):
                    after(last[g])
                    v.tensor_scalar(part(var, g), part(var, g), 1.0 / D, EPS, ALU.mult, ALU.add).then_inc(var_done, 1)

            def normed(g):
                v.wait_ge(rstd_done, g + 1)
                v.wait_ge(mean_done, g + 1)
                v.scalar_tensor_tensor(out=part(nmr, g), in0=part(mean, g), scalar=-1.0, in1=part(rstd, g),
                                       op0=ALU.mult, op1=ALU.mult).then_inc(nmr_done, 1)
                for b in range(g * GB, (g + 1) * GB, 2):
                    v.tensor_scalar(xn[:, b, :], xs[:, b, :], mean[:, b:b + 1], rstd[:, b:b + 1],
                                    ALU.subtract, ALU.mult).then_inc(xn_dve, 1)

            def low(e):
                low_gate_up(v, e)
                low_down(v, e).then_inc(w_lo_dve, 1)

            v.memset(b_rows[:].bitcast(I32), 0).then_inc(brow_zero, 1)
            v.memset(blk[:].rearrange("p g m b d -> p (g m b d)"), 0.0).then_inc(blk_zero, 1)
            v.memset(chosen[:, B, :], 0.0)
            v.memset(expert_i[:, T:T + 1], 0)
            for g in range(GN):
                v.wait_ge(x_in[g], 16)
                for b in range(g * GB, (g + 1) * GB):
                    ins = v.bn_stats(stats[:, b, :], xs[:, b, :])
                last[g] = mark(ins)
            for g in range(GN):
                moments(g)
            variances()

            def factor(product, a, c):
                for m in range(2):
                    ins = v.tensor_scalar(product[:, m, :], row[:, a, m, :], col[:, c + m:c + m + 1], None, ALU.mult)
                ins.then_inc(factors, 1)

            v.wait_ge(small_in, 16)
            factor(bqk, 0, 2)
            v.tensor_scalar(bq_sum[:], col[:, 2:4], float(P), None, ALU.mult).then_inc(factors, 1)
            factor(wqk, 0, 0)
            for g in range(GN):
                normed(g)

            def by_head(a):
                return a.unsqueeze(2).to_broadcast([D, 2, GB, HD])

            def flat(a, g):
                return a[:, g].rearrange("p m b j -> p (m b) j")

            def over(a, g):
                return a[:, g].unsqueeze(2).to_broadcast([D, 2 * GB, HD])

            for g in range(GN):
                v.wait_ge(g_ps, GB * (g + 1))
                v.tensor_copy(part(xsum, g).rearrange("p (k b) -> p k b", k=2), G[g][:, :, :, D]).then_inc(xsum_sb, 1)
                for h in (0, 1):
                    hs = slice(h * HD, (h + 1) * HD)
                    last[g] = mark(v.tensor_copy(gsel[hs, g * GB:(g + 1) * GB].rearrange("p (k b) j -> p k b j", k=2),
                                                 G[g][hs, :, :, hs]))
            v.wait_ge(factors, 3)
            for m in range(2):
                for g in range(GN):
                    v.wait_ge(xsum_sb, g + 1)
                    k = mark(v.tensor_scalar(part(qsum[:, m], g), part(xsum, g), col[:, m:m + 1], bq_sum[:, m:m + 1],
                                             ALU.mult, ALU.add))

            def scores(g):
                v.wait_ge(g_act, 2 * (g + 1))
                return v.tensor_tensor(s[:, g], part(gsel, g).unsqueeze(1).to_broadcast([D, 2, GB, HD]), by_head(wqk[:]), ALU.mult)

            both(scores)
            after(k)
            for g in range(GN):
                v.tensor_tensor(t2[:, g], qsum[:, :, g * GB:(g + 1) * GB].unsqueeze(3).to_broadcast([D, 2, GB, HD]),
                                by_head(row[:, 1]), ALU.mult).then_inc(t2_done, 1)

            def ctx_part(g):
                v.wait_ge(uq_done, g + 1)
                return v.tensor_tensor(s[:, g], s[:, g], uq[:, g], ALU.add)

            def sum_part(g):
                v.wait_ge(t2_done, g + 1)
                return v.tensor_tensor(s[:, g], s[:, g], t2[:, g], ALU.add)

            both(sum_part)
            both(ctx_part)
            both(lambda g: v.tensor_reduce(smax[:, g], flat(s, g), AX, ALU.max))
            for g in range(GN):
                after(last[g])
                v.tensor_tensor(flat(s, g), flat(s, g), over(smax, g), ALU.subtract).then_inc(s_done, 1)

            step(v.tensor_copy(b_part[:, 0], b_raw))
            rest = mark(v.tensor_tensor(b_rest[:, 0], b_raw, b_part[:, 0], ALU.subtract))

            def total(g):
                v.wait_ge(exp_done, g + 1)
                return v.tensor_reduce(rsum[:, g], flat(s, g), AX, ALU.add)

            both(total)
            both(lambda g: v.reciprocal(rsum[:, g], rsum[:, g]))
            both(lambda g: v.tensor_scalar(rsum[:, g], rsum[:, g], col[:, 4:5], 2.0, ALU.mult, ALU.mult))
            for g in range(GN):
                after(last[g])
                v.tensor_tensor(flat(s, g), flat(s, g), over(rsum, g), ALU.mult).then_inc(attn_done, 1)
            for g in range(GN):
                v.wait_ge(attn_done, g + 1)
                last[g] = mark(v.tensor_tensor(mv[:, g], s[:, g], by_head(row[:, 2]), ALU.mult))
            both(lambda g: v.tensor_tensor(mr[:, g, 0], mv[:, g, 0], mv[:, g, 1], ALU.add))
            for g in range(GN):
                v.wait_ge(r_done, g + 1)
                last[g] = mark(v.tensor_tensor(mr[:, g, 1], t2[:, g, 0], t2[:, g, 1], ALU.add))
                after(last[g])
                v.transpose(mrT[:, g].rearrange("p m b j -> p (m b j)"),
                            mr[:, g].rearrange("p m b j -> p (m b j)")).then_inc(mrT_done, 1)
            v.wait_ge(blk_zero, 1)
            for g in range(GN):
                v.wait_ge(mrT_done, g + 1)
                for h in (0, 1):
                    hs = slice(h * HD, (h + 1) * HD)
                    v.tensor_copy(blk[hs, g, :, :, hs].rearrange("p m b d -> p (m b) d"),
                                  mrT[hs, g].rearrange("p m b d -> p (m b) d")).then_inc(blk_dve, 1)
            v.wait_ge(ones_col, 3)
            k = mark(v.tensor_scalar(row_no[:], row_no[:], E - 1, None, ALU.bitwise_and))
            after(rest)
            rest = mark(v.tensor_copy(b_part[:, 1], b_rest[:, 0]))
            v.wait_ge(consts, 4)
            after(k)
            v.tensor_scalar(pick[:], tile_no[:, 0:E].unsqueeze(2).to_broadcast([P, E, P]), row_no[:, 0:1], None,
                            ALU.is_equal).then_inc(pick_done, 1)
            after(rest)
            step(v.tensor_tensor(b_rest[:, 1], b_rest[:, 0], b_part[:, 1], ALU.subtract))
            v.tensor_copy(b_part[:, 2], b_rest[:, 1]).then_inc(b_split, 1)
            for g in range(GN):
                for k in range(2):
                    v.wait_ge(att_ps, (1, 2, 3, 3)[2 * g + k])
                    for j in range(2):
                        ins = v.bn_stats(stats[:, g * GB + 2 * k + j, :], ATT[g][:, k, j, :])
                last[g] = mark(ins)
                moments(g)
                v.wait_ge(mean_done, GN + g + 1)
                v.tensor_tensor(pairs_of(xc, g), ATT[g],
                                part(mean, g).rearrange("p (k b) -> p k b", k=2).unsqueeze(3).to_broadcast([P, 2, 2, D]),
                                ALU.subtract).then_inc(xc_done, 1)
            variances()

            low_gate_up(v, 5)
            low_down(v, 5, slice(0, FC // 2))
            v.wait_ge(consts, N_CONST)
            v.wait_ge(logit_ps, GN)
            for g in range(GN):
                last[g] = mark(v.tensor_reduce(part(lmax, g), LOGIT[g], AX, ALU.max))
            for g in range(GN):
                after(last[g])
                v.tensor_tensor(part(logit, g), LOGIT[g], part(lmax, g).unsqueeze(2).to_broadcast([P, GB, E]),
                                ALU.subtract).then_inc(logit_sb, 1)
            ranks = rank_no[:].unsqueeze(1).to_broadcast([P, GB, E])

            def wide(a, g):
                return part(a, g).unsqueeze(2).to_broadcast([P, GB, E])

            for g in range(GN):
                v.wait_ge(logit_sb, g + 1)
                last[g] = mark(v.scalar_tensor_tensor(out=part(key, g), in0=part(logit, g), scalar=0.0, in1=ranks,
                                                      op0=ALU.is_equal, op1=ALU.mult))
            both(lambda g: v.tensor_reduce(part(kmax, g), part(key, g), AX, ALU.max))
            both(lambda g: v.tensor_tensor(part(mask[:, 0], g), part(key, g), wide(kmax, g), ALU.is_equal))
            both(lambda g: v.scalar_tensor_tensor(out=part(second, g), in0=part(mask[:, 0], g), scalar=-3.0e38,
                                                  in1=part(logit, g), op0=ALU.mult, op1=ALU.add))
            both(lambda g: v.tensor_reduce(part(lmax, g), part(second, g), AX, ALU.max))
            both(lambda g: v.tensor_tensor(part(key, g), part(second, g), wide(lmax, g), ALU.is_equal))
            both(lambda g: v.tensor_tensor(part(key, g), part(key, g), ranks, ALU.mult))
            both(lambda g: v.tensor_reduce(part(kmax, g), part(key, g), AX, ALU.max))
            both(lambda g: v.tensor_tensor(part(mask[:, 1], g), part(key, g), wide(kmax, g), ALU.is_equal))
            for g in range(GN):
                after(last[g])
                v.tensor_tensor(part(chosen, g), part(mask[:, 0], g), part(mask[:, 1], g), ALU.add).then_inc(chosen_done, 1)
            for g in range(GN):
                v.wait_ge(rstd_done, GN + g + 1)
                v.tensor_tensor(part(prob, g), part(logit, g), part(rstd, g).unsqueeze(2).to_broadcast([P, GB, E]),
                                ALU.mult).then_inc(scaled, 1)

            low_down(v, 5, slice(FC // 2, FC)).then_inc(w_lo_dve, 1)

            def lanes(i):
                v.tensor_tensor(lane_lhs[:, i], digit[:, 1, i * LG:(i + 1) * LG].unsqueeze(1).to_broadcast([P, P, LG]),
                                lane_rep[:], ALU.is_equal).then_inc(lane_done, 1)

            def by_choice(a):
                return a.unsqueeze(1).to_broadcast([P, K, B, E])

            v.wait_ge(place_ps, 1)
            k = mark(v.tensor_tensor(cmp[:], PLACE[:, B, :].unsqueeze(2).to_broadcast([P, E, B]),
                                     tile_edge[:].unsqueeze(1).to_broadcast([P, E, B]), ALU.is_gt))
            a = mark(v.tensor_tensor(prod[:], mask[:], by_choice(PLACE[:, 0:B, :]), ALU.mult))
            after(k)
            k = mark(v.tensor_reduce(ntile[:], cmp[:], AX, ALU.add))
            after(a)
            with nc.allow_low_precision(reason="whole numbers under 2^24"):
                a = mark(v.tensor_reduce(ahead_i[:].rearrange("p (k b) -> p k b", k=K), prod[:], AX, ALU.add))
            after(k)
            k = mark(v.tensor_tensor(cmp[:], lower[:], ntile[:].unsqueeze(1).to_broadcast([P, E, E]), ALU.mult))
            after(a)
            v.tensor_scalar(digit_i[:, 0], ahead_i[:], 7, None, ALU.logical_shift_right)
            a = mark(v.tensor_scalar(digit_i[:, 1], ahead_i[:], P - 1, None, ALU.bitwise_and))
            after(k)
            k = mark(v.tensor_reduce(first[:], cmp[:], AX, ALU.add))
            after(a)
            a = mark(v.tensor_copy(digit[:], digit_i[:]))
            after(k)
            k = mark(v.tensor_tensor(prod[:], mask[:], by_choice(first[:].unsqueeze(1).to_broadcast([P, B, E])), ALU.mult))
            after(a)
            lanes(0)
            after(k)
            with nc.allow_low_precision(reason="whole numbers under 2^11"):
                k = mark(v.tensor_reduce(start[:].rearrange("p (k b) -> p k b", k=K), prod[:], AX, ALU.add))
            past_done = mark(v.tensor_tensor(past[:], ntile[:], first[:], ALU.add))
            after(k)
            k = mark(v.tensor_tensor(digit[:, 0], digit[:, 0], start[:], ALU.add))
            lanes(1)
            after(k)
            v.tensor_tensor(in_tile[:], digit[:, 0].unsqueeze(1).to_broadcast([P, T, K * B]), tile_rep[:],
                            ALU.is_equal).then_inc(in_tile_done, 1)
            lanes(2)
            v.wait_ge(in_tile_done, 1)
            v.tensor_tensor(tile_rhs[:, 0], in_tile[:],
                            src_id[:].rearrange("p k b -> p (k b)").unsqueeze(1).to_broadcast([P, T, K * B]),
                            ALU.mult).then_inc(tile_rhs_done, 1)
            lanes(3)
            after(past_done)
            k = mark(v.tensor_tensor(cmp_t[:], tile_no[:].unsqueeze(2).to_broadcast([P, T, E]),
                                 past[:].unsqueeze(1).to_broadcast([P, T, E]), ALU.is_ge))
            v.wait_ge(inv_ps, 1)
            v.tensor_copy(src_i[:], INV[:, 0, :]).then_inc(src_done, 1)
            after(k)
            step(v.tensor_reduce(expert[:], cmp_t[:], AX, ALU.add))
            v.tensor_scalar(expert_i[:, 0:T], expert[:], E - 1.0, None, ALU.min).then_inc(experts_done, 1)
            k = mark(v.tensor_copy(dst[:], INV[:, 1, :]))
            low_gate_up(v, 6)
            after(k)
            mark(v.scalar_tensor_tensor(out=pad[:], in0=dst[:], scalar=0.0, in1=pad_row[:], op0=ALU.is_equal, op1=ALU.mult))
            k = mark(v.scalar_tensor_tensor(out=dst[:], in0=INV[:, 0, :], scalar=2.0, in1=dst[:], op0=ALU.mult, op1=ALU.add))
            low_down(v, 6).then_inc(w_lo_dve, 1)
            after(k)
            k = mark(v.tensor_tensor(dst[:], dst[:], pad[:], ALU.add))
            low_gate_up(v, 7, slice(F, 2 * F)).then_inc(w_lo_dve, 1)
            after(k)
            v.tensor_scalar(dst_i[:], dst[:], 1.0, None, ALU.subtract).then_inc(dst_done, 1)

            def turn(s, i, q):
                if real(s - 1):
                    v.wait_ge(hT_hi_done, s)
                    v.tensor_tensor(hT_lo[:, 1 - q], pH[1 - q], hT_hi[:, 1 - q].bitcast(F32),
                                    ALU.subtract).then_inc(hT_lo_done, 1)
                if real(s + 1):
                    e = expert_of(v, s + 1)
                if first_product(s):
                    low_down(v, 7).then_inc(w_lo_dve, 1)
                if real(s + 2):
                    v.wait_ge(xT_hi_done, s + 3)
                    v.tensor_tensor(xT_lo[:, q, :], pX, xT_hi[:, q, :].bitcast(F32), ALU.subtract).then_inc(xT_lo_done, 1)
                if real(s - 2):
                    v.wait_ge(y_ps, s - 1)
                    if again(s - 2) and not last_tile(s - 2):
                        v.wait_ge(scattered[q], (s - 2 - q) * 8)
                    results = pY_free if last_but_one(s - 2) else pY
                    v.tensor_reduce(y[:, 2 if last_tile(s - 2) else q, :], results.rearrange("p (c d) -> p d c", c=2),
                                    AX, ALU.add).then_inc(y_done, 1)
                if real(s + 1):
                    v.wait_ge(up_ps, s + 2)
                    v.tensor_tensor(hid[:, 1 - q, :], pU[1 - q], b_up[:, e, :], ALU.add).then_inc(up_done, 1)
                    v.wait_ge(act_done, s + 2)
                    v.wait_ge(up_done, s + 2)
                    v.tensor_tensor(hid[:, 1 - q, :], hid[:, 1 - q, :], act[:, 1 - q, :], ALU.mult).then_inc(hid_done, 1)

            v.wait_ge(b_up_in, 16)
            v.wait_ge(experts_done, 1)
            pipeline(v, turn)

            v.wait_ge(pexp_done, GN)
            step(v.tensor_reduce(psum_e[:], prob[:], AX, ALU.add))
            step(v.reciprocal(psum_e[:], psum_e[:]))
            step(v.tensor_tensor(prob[:], prob[:], psum_e[:].unsqueeze(2).to_broadcast([P, B, E]), ALU.mult))
            step(v.tensor_tensor(gated[:], mask[:], prob[:].unsqueeze(1).to_broadcast([P, K, B, E]), ALU.mult))
            v.tensor_reduce(gate[:], gated[:], AX, ALU.add).then_inc(gate_done, 1)
            v.wait_ge(gate_done, 1)
            for i in range(4):
                v.wait_ge(res_in[i], 16)
                for b in (2 * i, 2 * i + 1):
                    ins = v.scalar_tensor_tensor(out=fin[:, b, :], in0=res[:, b, 0, :], scalar=gate[:, 0, b:b + 1],
                                                 in1=x1[:, b, :], op0=ALU.mult, op1=ALU.add)
                ins.then_inc(first_added, 1)
            add_second(v, 2)
            add_second(v, 3)

        @block.tensor
        def _(pe):
            def warm(n, bank):
                for _ in range(n):
                    pe.matmul(ps[:, bank, :], ones_bf[:], ones_bf[:].unsqueeze(1).to_broadcast([P, 4, P]), start=True, stop=True)

            pe.wait_ge(ones_bf_done, 1)
            warm(10, 6)
            pe.wait_ge(ones_col, 3)
            pe.wait_ge(c_in, 16)

            def ctx_sums(g):
                pe.matmul(ps[:, 4 + g, :], ones[:], cn[:, g * GB:(g + 1) * GB, 0:D], start=True, stop=True).then_inc(csum_ps, 1)

            ctx_sums(0)
            for b in range(B):
                pe.wait_ge((xn_dve, xn_act)[b % 2], b // 2 + 1)
                pe.matmul(G[b // GB][:, b % GB // 2, b % 2, :], xn[:, b, :], cn[:, b, :], start=True, stop=True).then_inc(g_ps, 1)
            ctx_sums(1)
            pe.wait_ge(bp_in, 16)
            pe.wait_ge(ident_done, 1)
            pe.wait_ge(x_in[0], 16)
            pe.wait_ge(x_in[1], 16)
            for bank, b0, n in reversed(ATT_BANKS):
                if bank == 5:
                    warm(4, 6)
                    pe.wait_ge(csum_sb, 4)
                pe.matmul(ps[:, bank, 0:n * D], ones[0:1, :], bp[:].unsqueeze(1).to_broadcast([1, n, D]), start=True, stop=False)
                pe.matmul(ps[:, bank, 0:n * D], ident[:], xs[:, b0:b0 + n, :], start=False, stop=False)
            pe.wait_ge(cT_in, 16)
            pe.wait_ge(s_done, 1)
            warm(16, 6)
            for bank, b0, n in ATT_BANKS:
                g, j = b0 // GB, b0 % GB
                pe.wait_ge(blk_dve, 2 * (g + 1))
                pe.wait_ge(blk_act, 2 * (g + 1))
                pe.matmul(ps[:, bank, 0:n * D], ones[:], blk[:, g, 1, j:j + n, :], start=False, stop=False)
                for i in range(n):
                    mm = pe.matmul(ps[:, bank, i * D:(i + 1) * D], cT[:, b0 + i, :], blk[:, g, 0, j + i, :],
                                   start=False, stop=(i == n - 1))
                mm.then_inc(att_ps, 1)
            warm(3, 6)
            for g in range(GN):
                pe.wait_ge(xc_done, g + 1)
                for b in range(GB):
                    mm = pe.transpose(XCT[g * 2 + b // 2][:, b % 2, :], xc[:, g * GB + b, :], ident[:])
                    if b % 2 == 1:
                        mm.then_inc(xcT_ps, 1)
                warm(1, 2 - 2 * g)
                for b in range(GB):
                    if b % 2 == 0:
                        pe.wait_ge(xcT_sb, g * 2 + b // 2 + 1)
                    mm = pe.matmul(LOGIT[g][:, b, :], xcT[:, g * GB + b, :], rw[:], start=True, stop=True)
                mm.then_inc(logit_ps, 1)
            warm(9, 0)
            pe.wait_ge(consts, N_CONST)
            pe.wait_ge(chosen_done, GN)
            pe.wait_ge(x1_done, 1)
            pe.matmul(PLACE, before[:], chosen[:], start=True, stop=False)
            for b in range(B):
                mm = pe.matmul(PLACE[:, b + 1:B + 1, :], ones_bf[:],
                               chosen[:, b, :].unsqueeze(1).to_broadcast([P, B - b, E]), start=False, stop=(b == B - 1))
            mm.then_inc(place_ps, 1)
            pe.wait_ge(x1_done, GN)
            warm(14, 7)
            pe.wait_ge(tile_rhs_done, 1)
            pe.wait_ge(tile_rhs_act, K)
            for m in range(K * B):
                pe.wait_ge(lane_done, m // LG + 1)
                mm = pe.matmul(INV, lane_lhs[:, m // LG, :, m % LG], tile_rhs[:, :, :, m], start=(m == 0), stop=(m == K * B - 1))
            mm.then_inc(inv_ps, 1)
            warm(12, 7)

            pe.wait_ge(experts_done, 1)
            pe.wait_ge(brow_in, 16)
            pe.wait_ge(pick_done, 1)

            def turn(s, i, q):
                e_down = expert_of(pe, s - 2) if real(s - 2) else None
                if real(s - 1):
                    pe.wait_ge(hid_done, s)
                    for c in range(FC):
                        mm = pe.transpose(pH[1 - q][:, c, :], hid[:, 1 - q, c * P:(c + 1) * P], ident[:])
                    mm.then_inc(hT_ps, 1)
                if real(s - 2):
                    results = pY_free if last_but_one(s - 2) else pY
                    if last_but_one(s - 2):
                        pe.wait_ge(hT_lo_done, s - 1)
                    elif last_tile(s - 2):
                        pe.wait_ge(y_done, T - 2)
                        pe.wait_ge(hT_hi_done, T)
                    elif again(s - 1):
                        pe.wait_ge(y_done, s - 2)
                    else:
                        pe.wait_ge(w_lo_dve, 4)
                        pe.wait_ge(hT_lo_done, s - 1)
                    for c in range(FC):
                        pe.matmul(results, hT_hi[:, q, c, :], w_down[:, e_down, c].rearrange("p h d -> p (h d)"),
                                  start=(c == 0), stop=False)
                    if last_tile(s - 2):
                        pe.wait_ge(hT_lo_done, T)
                    for c in range(FC):
                        pe.matmul(results[:, 0:D], hT_lo[:, q, c, :], w_down[:, e_down, c, 0, :], start=False, stop=False)
                    pe.matmul(results[:, 0:D], pick[:, e_down, :], b_rows[:, F:BW], start=False, stop=True).then_inc(y_ps, 1)
                e = expert_of(pe, s + 1) if real(s + 1) else None
                if first_product(s):
                    pe.wait_ge(xT_hi_done, 1)
                    pe.matmul(pG[0], pick[:, e, :], b_rows[:, 0:F], start=True, stop=False)
                    pe.matmul(pG[0], xT_hi[:, 0, :], w_hi[:, e, 0:F], start=False, stop=False)
                    pe.matmul(pU[0], xT_hi[:, 0, :], w_hi[:, e, F:2 * F], start=True, stop=False)
                if real(s + 1) and not (real(s - 2) and again(s - 1)):
                    pe.wait_ge(xT_lo_done, s + 2)
                if real(s + 2):
                    x = (i + 2) % XG
                    pe.wait_ge(gathered[x], (s + 2 - x) * (16 // XG) + 16)
                    pe.transpose(pX, xg[:, x, :], ident[:]).then_inc(xT_ps, 1)
                if first_product(s):
                    pe.wait_ge(w_lo_pool, 6)
                    pe.wait_ge(w_lo_dve, 3)
                    for c0, psum, ready in ((0, pG[0], gate_ps), (F, pU[0], up_ps)):
                        pe.matmul(psum, xT_hi[:, 0, :], w_lo[:, e, c0:c0 + F], start=False, stop=False)
                        pe.matmul(psum, xT_lo[:, 0, :], w_hi[:, e, c0:c0 + F], start=False, stop=True).then_inc(ready, 1)
                elif real(s + 1):
                    pe.matmul(pG[1 - q], pick[:, e, :], b_rows[:, 0:F], start=True, stop=False)
                    for c0, psum, ready in ((0, pG[1 - q], gate_ps), (F, pU[1 - q], up_ps)):
                        pe.matmul(psum, xT_hi[:, 1 - q, :], w_lo[:, e, c0:c0 + F], start=(c0 > 0), stop=False)
                        pe.matmul(psum, xT_hi[:, 1 - q, :], w_hi[:, e, c0:c0 + F], start=False, stop=False)
                        pe.matmul(psum, xT_lo[:, 1 - q, :], w_hi[:, e, c0:c0 + F], start=False, stop=True).then_inc(ready, 1)

            pipeline(pe, turn)


def kernel(**inputs):
    import numpy as np
    import concourse.bacc as bacc
    from concourse.bass_utils import run_bass_kernel_spmd as run

    a = {k.replace("L0_xattn_", "").replace("L0_ffn_", ""): np.asarray(v) for k, v in inputs.items()}
    cols = np.stack([a[k] for k in ("wqg", "wql", "bqg", "bql", "wp")], axis=1)
    rows = np.stack([a[k].reshape(H, HD) for k in ("wkg", "wkl", "bkg", "bkl", "wvg", "wvl", "bvg", "bvl")], axis=1)
    rows = np.repeat(rows.reshape(H, 8 * HD), HD, axis=0)
    wpack = np.concatenate([
        a["wg_w"].transpose(2, 0, 1), a["w1_w"].transpose(2, 0, 1),
        a["w2_w"].reshape(E, D, FC, P).transpose(3, 0, 2, 1).reshape(P, E, FC * D)], axis=2)
    bias = np.concatenate([a["wg_b"], a["w2_b"]], axis=1)
    arrays = {
        "x": a["x"], "ctxn": a["ctx_1024"], "ctxT": a["ctx_1024"].transpose(2, 0, 1),
        "small_pack": np.concatenate([rows, cols, a["router_w"].T, bias.reshape(P, E * BW // P)], axis=1),
        "bp_row": a["bp"].reshape(1, D), "up_bias": a["w1_b"], "wpack": wpack,
    }
    arrays = {k: np.ascontiguousarray(v) for k, v in arrays.items()}
    nc = bacc.Bacc("TRN2", target_bir_lowering=False, num_devices=1)
    args = [nc.dram_tensor(k, v.shape, F32, kind="ExternalInput").ap() for k, v in arrays.items()]
    out = nc.dram_tensor("out", (B, P, D), F32, kind="ExternalOutput").ap()
    program(nc, *args, out)
    r = run(nc, [arrays], core_ids=[0])
    return r.results[0]["out"]
```
